# Optimizing a Trainium2 kernel written in Bass

```python
import numpy as np
import jax
import jax.numpy as jnp

def _softmax(x, axis=-1):
    return jax.nn.softmax(x, axis=axis)

def _gelu(x):
    return jax.nn.gelu(x, approximate=True)

def _silu(x):
    return jax.nn.silu(x)

def _sigmoid(x):
    return jax.nn.sigmoid(x)

def _layernorm(x, axis=-1, eps=1e-05):
    m = jnp.mean(x, axis=axis, keepdims=True)
    v = jnp.var(x, axis=axis, keepdims=True)
    return (x - m) / jnp.sqrt(v + eps)

def _scatter_add(tgt, idx, src, axis=0):
    return tgt.at[idx].add(src)

def _segment_sum(src, seg, n):
    return jax.ops.segment_sum(src, seg, n)
kernel_name = 'mk_gnn_preln_d1_gnn_r16_d8cdef'

def setup_inputs(seed: int=0):
    np.random.seed(seed)
    _w = jnp.asarray

    def _rec_inputs():
        import jax
        import jax.numpy as jnp
        _gk = jax.random.key(seed)
        x = -0.0002117 + 1 * jax.random.normal(jax.random.fold_in(_gk, 1), (625, 512), jnp.float32)
        _s = jax.random.randint(jax.random.fold_in(_gk, 2), (10000,), 0, 625, jnp.int32)
        _d = jax.random.randint(jax.random.fold_in(_gk, 3), (10000,), 0, 625, jnp.int32)
        _loop = jnp.arange(625, dtype=jnp.int32)
        src = jnp.concatenate([_s, _d, _loop])
        dst = jnp.concatenate([_d, _s, _loop])
        _o = jnp.argsort(dst, stable=True)
        src = src[_o]
        dst = dst[_o]
        edge_type_4 = jax.random.randint(jax.random.fold_in(_gk, 12), (20625,), 0, 4, jnp.int32)
        edge_weight = jax.random.uniform(jax.random.fold_in(_gk, 13), (20625,), jnp.float32, 0.0, 0.999995)
        return (x, src, dst, edge_type_4, edge_weight)
    x, src, dst, edge_type_4, edge_weight = _rec_inputs()

    def _L0_gnn_setup():
        import jax, jax.numpy as jnp
        import numpy as np
        DIM = 512
        NUM_REL = 4
        N_NODES = 3125
        N_EDGES = 10000

        def _layer_norm(x, g, b, eps=1e-05):
            mu = jnp.mean(x, axis=-1, keepdims=True)
            var = jnp.mean((x - mu) ** 2, axis=-1, keepdims=True)
            return (x - mu) * jax.lax.rsqrt(var + eps) * g + b
        key = jax.random.key(seed)
        ks = jax.random.split(key, 16)
        s = 1.0 / np.sqrt(DIM)
        inp = {'x': jax.random.normal(ks[0], (N_NODES, DIM), jnp.float32), 'edge_index': jax.random.randint(ks[1], (2, N_EDGES), 0, N_NODES, jnp.int32), 'edge_type': jax.random.randint(ks[2], (N_EDGES,), 0, NUM_REL, jnp.int32), 'edge_weight': jax.random.uniform(ks[3], (N_EDGES,), jnp.float32), 'W_self': jax.random.uniform(ks[4], (DIM, DIM), jnp.float32, -s, s), 'b_self': jnp.zeros((DIM,), jnp.float32), 'W_rel': jax.random.uniform(ks[5], (NUM_REL, DIM, DIM), jnp.float32, -s, s), 'b_rel': jnp.zeros((NUM_REL, DIM), jnp.float32), 'ln1_g': jnp.ones((DIM,), jnp.float32), 'ln1_b': jnp.zeros((DIM,), jnp.float32), 'ln2_g': jnp.ones((DIM,), jnp.float32), 'ln2_b': jnp.zeros((DIM,), jnp.float32), 'W_ffn1': jax.random.uniform(ks[6], (DIM, 2 * DIM), jnp.float32, -s, s), 'b_ffn1': jnp.zeros((2 * DIM,), jnp.float32), 'W_ffn2': jax.random.uniform(ks[7], (2 * DIM, DIM), jnp.float32, -1.0 / np.sqrt(2 * DIM), 1.0 / np.sqrt(2 * DIM)), 'b_ffn2': jnp.zeros((DIM,), jnp.float32)}
        return inp
    _L0_gnn_all = _L0_gnn_setup()
    _L0_gnn_in = {k: v for k, v in _L0_gnn_all.items() if k in ('W_self', 'b_self', 'W_rel', 'b_rel', 'ln1_g', 'ln1_b', 'ln2_g', 'ln2_b', 'W_ffn1', 'b_ffn1', 'W_ffn2', 'b_ffn2')}
    del _L0_gnn_all
    return {'x': x, 'src': src, 'dst': dst, 'edge_type_4': edge_type_4, 'edge_weight': edge_weight, 'L0_gnn_W_self': _L0_gnn_in['W_self'], 'L0_gnn_b_self': _L0_gnn_in['b_self'], 'L0_gnn_W_rel': _L0_gnn_in['W_rel'], 'L0_gnn_b_rel': _L0_gnn_in['b_rel'], 'L0_gnn_ln1_g': _L0_gnn_in['ln1_g'], 'L0_gnn_ln1_b': _L0_gnn_in['ln1_b'], 'L0_gnn_ln2_g': _L0_gnn_in['ln2_g'], 'L0_gnn_ln2_b': _L0_gnn_in['ln2_b'], 'L0_gnn_W_ffn1': _L0_gnn_in['W_ffn1'], 'L0_gnn_b_ffn1': _L0_gnn_in['b_ffn1'], 'L0_gnn_W_ffn2': _L0_gnn_in['W_ffn2'], 'L0_gnn_b_ffn2': _L0_gnn_in['b_ffn2']}

def reference(x, src, dst, edge_type_4, edge_weight, L0_gnn_W_self, L0_gnn_b_self, L0_gnn_W_rel, L0_gnn_b_rel, L0_gnn_ln1_g, L0_gnn_ln1_b, L0_gnn_ln2_g, L0_gnn_ln2_b, L0_gnn_W_ffn1, L0_gnn_b_ffn1, L0_gnn_W_ffn2, L0_gnn_b_ffn2):
    import jax
    import jax.numpy as jnp

    def _L0_gnn_ref(x, edge_index, edge_type, edge_weight, W_self, b_self, W_rel, b_rel, ln1_g, ln1_b, ln2_g, ln2_b, W_ffn1, b_ffn1, W_ffn2, b_ffn2):
        import jax, jax.numpy as jnp
        import numpy as np
        DIM = 512
        NUM_REL = 4
        N_NODES = 3125
        N_EDGES = 10000

        def _layer_norm(x, g, b, eps=1e-05):
            mu = jnp.mean(x, axis=-1, keepdims=True)
            var = jnp.mean((x - mu) ** 2, axis=-1, keepdims=True)
            return (x - mu) * jax.lax.rsqrt(var + eps) * g + b
        n = x.shape[0]
        src, dst = (edge_index[0], edge_index[1])
        xs = x[src]
        total_msg = jnp.zeros_like(xs)
        for r in range(NUM_REL):
            w_r = jnp.where(edge_type == r, edge_weight, 0.0)
            total_msg = total_msg + (xs @ W_rel[r] + b_rel[r]) * w_r[:, None]
        agg = jax.ops.segment_sum(total_msg, dst, num_segments=n)
        deg = jax.ops.segment_sum(edge_weight, dst, num_segments=n)
        agg = agg / jnp.maximum(deg, 1.0)[:, None]
        h = x @ W_self + b_self + agg
        x1 = _layer_norm(x + h, ln1_g, ln1_b)
        ffn = jax.nn.gelu(x1 @ W_ffn1 + b_ffn1, approximate=False) @ W_ffn2 + b_ffn2
        out = _layer_norm(x1 + ffn, ln2_g, ln2_b)
        return out
    edge_index = jnp.stack([src, dst])
    h = jnp.maximum(_layernorm(x, axis=-1), 0.0)
    x = x + _L0_gnn_ref(h, edge_index, edge_type_4, edge_weight, L0_gnn_W_self, L0_gnn_b_self, L0_gnn_W_rel, L0_gnn_b_rel, L0_gnn_ln1_g, L0_gnn_ln1_b, L0_gnn_ln2_g, L0_gnn_ln2_b, L0_gnn_W_ffn1, L0_gnn_b_ffn1, L0_gnn_W_ffn2, L0_gnn_b_ffn2)
    return x

_drawn_inputs = setup_inputs


def setup_inputs(seed=0):
    import zlib

    import numpy as np

    out = dict(_drawn_inputs(seed))
    spreads = {'L0_gnn_b_self': (0.0, 0.1),
     'L0_gnn_b_rel': (0.0, 0.1),
     'L0_gnn_ln1_g': (1.0, 0.2),
     'L0_gnn_ln1_b': (0.0, 0.1),
     'L0_gnn_ln2_g': (1.0, 0.2),
     'L0_gnn_ln2_b': (0.0, 0.1),
     'L0_gnn_b_ffn1': (0.0, 0.417),
     'L0_gnn_b_ffn2': (0.0, 0.1)}
    factors = {}
    for name, (base, spread) in spreads.items():
        noise = np.random.default_rng([zlib.crc32(name.encode()), seed]).standard_normal(out[name].shape)
        drawn = base * np.exp(spread * noise) if base else spread * noise
        out[name] = jnp.asarray(drawn.astype(out[name].dtype))
    for name, factor in factors.items():
        out[name] = (out[name] * factor).astype(out[name].dtype)
    return out
```

```python
from contextlib import ExitStack

import concourse.bass as bass
from concourse import mybir


F32 = mybir.dt.float32
F32R = mybir.dt.float32r
F16 = mybir.dt.float16
I32 = mybir.dt.int32
ALU = mybir.AluOpType
ACT = mybir.ActivationFunctionType
AX = mybir.AxisListType

P = 128
LO_SCALE = 4096.0
EPS = 1e-5


def gnn_layer(nc, x, src, dst, etype, ew, W_self, b_self, W_rel, b_rel, ln1_g, ln1_b, ln2_g, ln2_b,
              W1, b1, W2, b2, out):
    N, D = x.shape
    E = src.shape[0]
    R = W_rel.shape[0]
    F = W1.shape[1]
    KD = D // P
    KF = F // P
    NT = -(-N // P)
    NP = NT * P
    ROWS = [min(P, N - c * P) for c in range(NT)]
    ET = -(-E // P)
    ETB = ET - P
    ELAST = E - (ET - 1) * P
    BW = 16
    BC = BW * R
    NB = NP // BW
    HB = 4
    HC = HB * BC
    HD = HB * BW
    NQ = NB // HB
    SL = 6
    RING = 2 * SL
    UC = 1024
    FG = [(0, 3 * P), (3 * P, NP - 3 * P)]

    base = nc.sbuf_base + (-nc.sbuf_base) % 64

    def sb(name, shape, dt, kb):
        return nc.alloc_sbuf_tensor_at(name, shape, dt, offset=base + int(kb * 1024))

    wrel_hi = sb("wrel_hi", [P, R, KD, D], F32R, 0)
    wrel_lo = sb("wrel_lo", [P, R, KD, D], F32R, 32)
    wself_hi = sb("wself_hi", [P, KD, D], F32R, 64)
    wself_lo = sb("wself_lo", [P, KD, D], F32R, 72)
    x1T_hi = sb("x1T_hi", [P, KD, NP], F32R, 64)
    x1T_lo = sb("x1T_lo", [P, KD, NP], F32R, 74)
    onehot = sb("onehot", [P, RING, NP], F16, 84)
    wkey = sb("wkey", [P, RING, 2 * BC], F16, 99)
    AT_hi = sb("AT_hi", [P, 2, NT, HC], F32R, 102)
    AT_lo = sb("AT_lo", [P, 2, NT, HC], F32R, 112)
    A32 = sb("A32", [P, NT, HC], F32, 122)
    G_hi = sb("G_hi", [P, KD, R, P], F32R, 127)
    G_lo = sb("G_lo", [P, KD, R, P], F32R, 135)
    h32 = sb("h32", [P, NT, D], F32, 127)
    hT = [sb("hT0", [P, 2, KD, P], F32R, 122), sb("hT1", [P, 2, KD, P], F32R, 137)]
    h_hi = sb("h_hi", [P, NT, D], F32R, 143)
    h_lo = sb("h_lo", [P, NT, D], F32R, 153)
    x1 = sb("x1", [P, NT, D], F32, 163)
    bself_bc = sb("bself_bc", [P, D], F32, 173)
    g1_bc = sb("g1_bc", [P, D], F32, 175)
    b1_bc = sb("b1_bc", [P, D], F32, 177)
    stage = sb("stage", [P, 3, UC], F32, 179)
    fields = sb("fields", [P, 4, ET], F32, 191)
    iota_src = sb("iota_src", [P, NP], F16, 193.75)
    iota_key = sb("iota_key", [P, BC], F16, 195)
    zeros = sb("zeros", [P, 64], F16, 195.125)
    ident = sb("ident", [P, P], F32, 195.25)
    ones = sb("ones", [P, P], F32, 195.75)
    key_off = sb("key_off", [P, NB, 4], F32, 196.25)
    slot = sb("slot", [P, 2, 4, SL], F32, 197)
    A_sum = sb("A_sum", [P, HC], F32, 197.25)
    brel_sb = sb("brel_sb", [R, D], F32, 198.25)
    tbuf = sb("tbuf", [P, D], F32, 200.25)
    xhat = sb("xhat", [P, D], F32, 202.25)
    D4 = sb("D4", [R, P], F32, 204.25)
    small = sb("small", [P, 160], F32, 204.75)
    mask_r = sb("mask_r", [R, HC], F32, 205.5)
    f_i32 = sb("f_i32", [P, NB + 8], I32, 206.5)
    dm = sb("dm", [R, HC], F32, 206.75)
    gkey = wkey[:, 0:4, :].rearrange("p s n -> p (s n)")
    rawA = sb("rawA", [P, 4, P], I32, 102)
    rawB = sb("rawB", [P, 4, P], I32, 104)
    TF = [sb("TFA", [P, 4, P], F32, 106), sb("TFB", [P, 4, P], F32, 108)]
    w16 = [sb("w16A", [P, P], F16, 110), sb("w16B", [P, P], F16, 110.5)]
    iota_blk = sb("iota_blk", [P, NB], F32, 111)
    ind = sb("ind", [P, 2, NB], F32, 111.5)
    ov = sb("ov", [P, 2, NB], F32, 112)
    uu = sb("uu", [P, 2, NB], F32, 112.5)
    u2 = sb("u2", [P, 2, NB], F32, 113)
    vv = sb("vv", [P, 2, NB], F32, 113.5)
    fcol = sb("fcol", [P, NB], F32, 114)
    iota_i = sb("iota_i", [P, 64], I32, 114.5)
    W1_hi = sb("W1_hi", [P, KD, F], F32R, 84)
    W1_lo = sb("W1_lo", [P, KD, F], F32R, 102)
    W2_hi = sb("W2_hi", [P, KF, D], F32R, 143)
    W2_lo = sb("W2_lo", [P, KF, D], F32R, 127)
    u_hi = sb("u_hi", [P, KF, NP], F32R, 0)
    u_lo = sb("u_lo", [P, KF, NP], F32R, 20)
    u32 = sb("u32", [P, 2, 3 * P], F32, 40)
    x_again = sb("x_again", [P, NT, D], F32, 44)
    g2_bc = sb("g2_bc", [P, D], F32, 54)
    b2_bc = sb("b2_bc", [P, D], F32, 56)
    bf2_bc = sb("bf2_bc", [P, D], F32, 58)
    ybuf = sb("ybuf", [P, 2, D], F32, 60)
    t2buf = sb("t2buf", [P, 2, D], F32, 122)

    stats = small[:, 0:30].rearrange("p (c s) -> p c s", s=6)
    mv = small[:, 30:40].rearrange("p (c s) -> p c s", s=2)
    rstd = small[:, 40:45]
    nmr = small[:, 45:50]
    mhalf = small[:, 50:55]
    var_e = small[:, 55:60]
    rdeg = small[:, 60:65]
    dmin = small[:, 65:67]
    dmax = small[:, 67:69]
    dminm = small[:, 69:71]
    negt = small[:, 71:73]
    vsum = small[:, 73:75]
    bf1 = small[:, 76:76 + KF]
    st1 = small[:, 84:90]
    mv1 = small[:, 90:92]
    ve1 = small[:, 92:93]
    rs1 = small[:, 93:94]
    nm1 = small[:, 94:95]
    st2 = small[:, 100:112].rearrange("p (c s) -> p c s", s=6)
    mv2 = small[:, 112:116].rearrange("p (c s) -> p c s", s=2)
    ve2 = small[:, 116:118]
    rs2 = small[:, 118:120]
    nm2 = small[:, 120:122]

    gslot = small[:, 124:128]

    psA = nc.alloc_psum_tensor("psA", [P, NT, 512], F32)
    psG = nc.alloc_psum_tensor("psG", [P, 2, 512], F32)
    psX = nc.alloc_psum_tensor("psX", [P, 512], F32)
    psGk = psG[:, :, :].rearrange("p b (k n) -> p (b k) n", k=2)

    ctx = ExitStack()
    with ctx:
        def sem(name):
            return ctx.enter_context(nc.semaphore(name))

        edges_in = sem("edges_in")
        x_in = [sem(f"x_in{c}") for c in range(NT)]
        consts_in = sem("consts_in")
        stage_in = [sem(f"stage_in{i}") for i in range(3)]
        late_in = sem("late_in")
        out_done = [sem(f"out_done{i}") for i in range(2)]
        iotas = sem("iotas")
        pads = sem("pads")
        dchain = sem("dchain")
        pchain = sem("pchain")
        efields = sem("efields")
        eT = sem("eT")
        find = sem("find")
        fcnt = sem("fcnt")
        viol = sem("viol")
        vcnt = sem("vcnt")
        regs_in = sem("regs_in")
        xstat = sem("xstat")
        xrstd = sem("xrstd")
        xnmr = sem("xnmr")
        h_act = sem("h_act")
        h_los = sem("h_los")
        h_bs = sem("h_bs")
        w_hi = sem("w_hi")
        w_lo = sem("w_lo")
        hT_ps = sem("hT_ps")
        hT_a = sem("hT_a")
        hT_b = sem("hT_b")
        self_ps = sem("self_ps")
        self_ev = sem("self_ev")
        gath = sem("gath")
        blk_in = sem("blk_in")
        blk_used = sem("blk_used")
        gen_in = sem("gen_in")
        gen_m = sem("gen_m")
        gen_used = sem("gen_used")
        A_ps = sem("A_ps")
        A_lo_ev = sem("A_lo_ev")
        A_ev = sem("A_ev")
        AT_a = sem("AT_a")
        AT_b = sem("AT_b")
        A_s = sem("A_s")
        G_ps = sem("G_ps")
        G_a = sem("G_a")
        G_b = sem("G_b")
        D_ps = sem("D_ps")
        D_m = sem("D_m")
        D_ev = sem("D_ev")
        deg_ps = sem("deg_ps")
        deg_m = sem("deg_m")
        deg_ev = sem("deg_ev")
        W_ps = sem("W_ps")
        t_out = sem("t_out")
        ln1_s = sem("ln1_s")
        ln1_v = sem("ln1_v")
        ln1_r = sem("ln1_r")
        ln1_n = sem("ln1_n")
        xhat_in = sem("xhat_in")
        x1_in = sem("x1_in")
        xT_ps = sem("xT_ps")
        xT_a = sem("xT_a")
        xT_b = sem("xT_b")
        U_ps = sem("U_ps")
        U_g = sem("U_g")
        U_a = sem("U_a")
        U_b = sem("U_b")
        x1b = sem("x1b")
        Y_ps = sem("Y_ps")
        Y_ev = sem("Y_ev")
        ln2_v = sem("ln2_v")
        ln2_r = sem("ln2_r")
        ln2_n = sem("ln2_n")
        y_hat = sem("y_hat")
        y_out = sem("y_out")

        block = ctx.enter_context(nc.Block())

        units = []
        for k in range(0, KD, 2):
            units.append((W_self.rearrange("(k p) n -> p k n", p=P)[:, k:k + 2, :],
                          wself_hi[:, k:k + 2, :], wself_lo[:, k:k + 2, :]))
        for r in range(R):
            for k in range(0, KD, 2):
                units.append((W_rel[r].rearrange("(k p) n -> p k n", p=P)[:, k:k + 2, :],
                              wrel_hi[:, r, k:k + 2, :], wrel_lo[:, r, k:k + 2, :]))
        U_SELF, U_REL = 2, 2 + 2 * R
        for k in range(KD):
            units.append((W1[k * P:(k + 1) * P, :], W1_hi[:, k, :], W1_lo[:, k, :]))
        U_W1 = U_REL + KD
        for k in range(0, KF, 2):
            units.append((W2.rearrange("(k p) n -> p k n", p=P)[:, k:k + 2, :],
                          W2_hi[:, k:k + 2, :], W2_lo[:, k:k + 2, :]))
        NU = len(units)

        def stage_view(u):
            v = stage[:, u % 3, :]
            return v if U_REL <= u < U_W1 else v.rearrange("p (k n) -> p k n", k=2)

        def f32(ap):
            return ap.bitcast(F32)

        def ybank(c):
            return [psG[:, 0, :], psG[:, 1, :], psX[:, :]][c % 3]

        def low_part(eng, u):
            eng.wait_ge(w_hi, u + 1)
            v, hi, lo = stage_view(u), units[u][1], units[u][2]
            if u == U_REL:
                eng.wait_ge(G_ps, NQ)
            nc.gpsimd.tensor_tensor(lo, v, f32(hi), ALU.subtract).then_inc(w_lo, 1)

        def ln1_pool(c):
            g, pool, m = nc.gpsimd, nc.gpsimd, ROWS[c]
            pool.wait_ge(ln1_v, c + 1)
            g.tensor_scalar(ve1[0:m], mv1[0:m, 1:2], EPS, None, ALU.add).then_inc(ln1_s, 1)
            pool.wait_ge(ln1_s, 2 * c + 1)
            g.tensor_tensor(rs1[0:m], ve1[0:m], mhalf[0:m, 0:1], ALU.pow).then_inc(ln1_r, 1)
            pool.wait_ge(xhat_in, c + 1)
            g.tensor_tensor(xhat[0:m, :], xhat[0:m, :], g1_bc[0:m, :], ALU.mult).then_inc(ln1_s, 1)
            pool.wait_ge(ln1_s, 2 * c + 2)
            g.tensor_tensor(x1[0:m, c, :], xhat[0:m, :], b1_bc[0:m, :], ALU.add).then_inc(x1_in, 1)

        def ln1_act(c):
            a, m = nc.scalar, ROWS[c]
            a.wait_ge(ln1_n, c + 1)
            if c >= 1:
                a.wait_ge(x1_in, c)
            a.activation(xhat[0:m, :], tbuf[0:m, :], ACT.Identity, scale=rs1[0:m], bias=nm1[0:m]).then_inc(xhat_in, 1)

        def turn_act(c):
            a, m = nc.scalar, ROWS[c]
            a.wait_ge(xT_ps, c + 1)
            a.copy(x1T_hi[:, :, c * P:c * P + m],
                   psX[:, :].rearrange("p (k m) -> p k m", k=KD)[:, :, 0:m]).then_inc(xT_a, 1)

        @block.sync
        def _(sp):
            for c in range(NT):
                sp.dma_start(h32[0:ROWS[c], c, :], x[c * P:c * P + ROWS[c], :]).then_inc(x_in[c], 16)
                if c == 0:
                    for u in range(3):
                        sp.dma_start(stage_view(u), units[u][0]).then_inc(stage_in[u % 3], 16)
            for u in range(3, NU):
                sp.wait_ge(w_lo, u - 2)
                sp.dma_start(stage_view(u), units[u][0]).then_inc(stage_in[u % 3], 16)
            sp.wait_ge(W_ps, NT)
            for c in range(NT):
                sp.dma_start(x_again[0:ROWS[c], c, :], x[c * P:c * P + ROWS[c], :]).then_inc(late_in, 16)
            for buf, v in ((g2_bc, ln2_g), (b2_bc, ln2_b), (bf2_bc, b2)):
                sp.dma_start(buf[:, :], v.rearrange("(a d) -> a d", a=1).broadcast_to([P, D])).then_inc(late_in, 16)
            for c in range(NT):
                sp.wait_ge(y_out, c + 1)
                sp.dma_start(out[c * P:c * P + ROWS[c], :], ybuf[0:ROWS[c], c % 2, :]).then_inc(out_done[c % 2], 16)
            for i in range(2):
                sp.wait_ge(out_done[i], 16 * len(range(i, NT, 2)))

        @block.gpsimd
        def _(pool):
            chain = [0]

            def link(ins):
                chain[0] += 1
                ins.then_inc(pchain, 1)
                pool.wait_ge(pchain, chain[0])

            g = nc.gpsimd
            g.iota(iota_src[:, :], [[1, NP]], base=0, channel_multiplier=0, allow_small_or_imprecise_dtypes=True)
            g.iota(iota_key[:, :], [[1, BC]], base=0, channel_multiplier=0, allow_small_or_imprecise_dtypes=True)
            g.iota(iota_blk[:, :], [[BW, NB]], base=0, channel_multiplier=0, allow_small_or_imprecise_dtypes=True)
            g.iota(negt, [[-P, 2]], base=0, channel_multiplier=-1, allow_small_or_imprecise_dtypes=True)
            g.memset(ones[:, :], 1.0)
            link(g.memset(key_off[:, :, :], 0.0))
            g.iota(key_off[:, :, 1], [[BC, NB]], base=0, channel_multiplier=0, allow_small_or_imprecise_dtypes=True)
            g.memset(mhalf, -0.5)
            link(g.memset(ident[:, :], 0.0))
            g.affine_select(out=ident[:, :], in_=ident[:, :], compare_op=ALU.not_equal, fill=1.0, base=0,
                            pattern=[[-1, P]], channel_multiplier=1)
            link(g.memset(mask_r[:, :], 0.0))
            link(g.affine_select(out=mask_r[:, :].rearrange("k (d r) -> k d r", r=R),
                                 in_=mask_r[:, :].rearrange("k (d r) -> k d r", r=R),
                                 compare_op=ALU.not_equal, fill=1.0, base=0,
                                 pattern=[[0, HD], [-1, R]], channel_multiplier=1))
            g.memset(zeros[:, :], 0.0).then_inc(iotas, 1)
            pool.wait_ge(xstat, NT)
            link(g.tensor_scalar(var_e, mv[:, :, 1], EPS, None, ALU.add))
            g.tensor_tensor(rstd, var_e, mhalf, ALU.pow).then_inc(xrstd, 1)
            pool.wait_ge(consts_in, 16 * 6)
            for c in range(NT):
                m = ROWS[c]
                pool.wait_ge(h_act, 2 * (c + 1))
                g.tensor_tensor(h_lo[0:m, c, :], h32[0:m, c, :], f32(h_hi[0:m, c, :]), ALU.subtract).then_inc(h_los, 1)
                g.tensor_tensor(x1[0:m, c, :], h32[0:m, c, :], bself_bc[0:m, :], ALU.add).then_inc(h_bs, 1)
                for u in (2 * c, 2 * c + 1):
                    low_part(pool, u)
            for q in range(NQ):
                pool.wait_ge(AT_a, q + 1)
                if q >= 2:
                    pool.wait_ge(G_ps, q - 1)
                g.tensor_tensor(AT_lo[:, q % 2, :, :], A32[:, :, :], f32(AT_hi[:, q % 2, :, :]), ALU.subtract).then_inc(AT_b, 1)
                if q >= 1:
                    pool.wait_ge(D_ps, q)
                link(g.tensor_tensor(A_sum[:, :], A32[:, 0, :], A32[:, 1, :], ALU.add))
                for s in range(2, NT):
                    i = g.tensor_tensor(A_sum[:, :], A_sum[:, :], A32[:, s, :], ALU.add)
                    if s < NT - 1:
                        link(i)
                i.then_inc(A_s, 1)
                if q % 2 == 0 and q >= 2:
                    ln1_pool(q // 2 - 1)
            for u in range(U_REL, U_W1):
                low_part(pool, u)
            ln1_pool(NT - 1)
            pool.wait_ge(W_ps, NT)
            for u in range(U_W1, NU):
                low_part(pool, u)
            pool.wait_ge(late_in, 16 * (NT + 3))
            for c in range(NT):
                m = ROWS[c]
                pool.wait_ge(xT_ps, c + 1)
                g.tensor_tensor(x1[0:m, c, :], x1[0:m, c, :], bf2_bc[0:m, :], ALU.add).then_inc(x1b, 1)
            for c in range(NT):
                m, b = ROWS[c], c % 2
                pool.wait_ge(ln2_v, c + 1)
                link(g.tensor_scalar(ve2[0:m, b:b + 1], mv2[0:m, b, 1:2], EPS, None, ALU.add))
                g.tensor_tensor(rs2[0:m, b:b + 1], ve2[0:m, b:b + 1], mhalf[0:m, 0:1], ALU.pow).then_inc(ln2_r, 1)
                pool.wait_ge(y_hat, c + 1)
                link(g.tensor_tensor(t2buf[0:m, b, :], t2buf[0:m, b, :], g2_bc[0:m, :], ALU.mult))
                link(g.tensor_tensor(x_again[0:m, c, :], x_again[0:m, c, :], b2_bc[0:m, :], ALU.add))
                if c >= 2:
                    pool.wait_ge(out_done[b], 16 * (c // 2))
                g.tensor_tensor(ybuf[0:m, b, :], t2buf[0:m, b, :], x_again[0:m, c, :], ALU.add).then_inc(y_out, 1)

        @block.scalar
        def _(act):
            a = nc.scalar
            act.wait_ge(pads, 1)
            full = P * P
            mid = (ET - 1) * P
            for i, v in enumerate((src, dst, etype, ew)):
                v = v.bitcast(I32) if i == 3 else v
                act.dma_start(rawA[:, i, :], v[0:full].rearrange("(t e) -> t e", e=P)).then_inc(edges_in, 16)
                act.dma_start(rawB[0:ETB - 1, i, :], v[full:mid].rearrange("(t e) -> t e", e=P)).then_inc(edges_in, 16)
                act.dma_start(rawB[ETB - 1:ETB, i, 0:ELAST], v[mid:E].rearrange("(t e) -> t e", t=1)).then_inc(edges_in, 16)
            for buf, v in ((bself_bc, b_self), (g1_bc, ln1_g), (b1_bc, ln1_b)):
                act.dma_start(buf[:, :], v.rearrange("(a d) -> a d", a=1).broadcast_to([P, D])).then_inc(consts_in, 16)
            act.dma_start(brel_sb[:, :], b_rel).then_inc(consts_in, 16)
            with nc.allow_non_contiguous_dma("bias by partition"):
                act.dma_start(bf1[:, 0:KF // 2], b1.rearrange("(f p) -> p f", p=P)[:, 0:KF // 2]).then_inc(consts_in, 16)
                act.dma_start(bf1[:, KF // 2:KF], b1.rearrange("(f p) -> p f", p=P)[:, KF // 2:KF]).then_inc(consts_in, 16)

            def high_part(u):
                act.wait_ge(stage_in[u % 3], 16 * (u // 3 + 1))
                if u == U_REL:
                    act.wait_ge(blk_used, NB)
                if u == U_W1:
                    act.wait_ge(G_ps, NQ)
                a.copy(units[u][1], stage_view(u)).then_inc(w_hi, 1)

            high_part(0)
            high_part(1)
            act.wait_ge(xnmr, 1)
            for c in range(NT):
                m = ROWS[c]
                a.activation(h_hi[0:m, c, :], h32[0:m, c, :], ACT.Relu, scale=rstd[0:m, c:c + 1],
                             bias=nmr[0:m, c:c + 1]).then_inc(h_act, 1)
                act.wait_ge(h_act, 2 * c + 1)
                a.activation(h32[0:m, c, :], h32[0:m, c, :], ACT.Relu, scale=rstd[0:m, c:c + 1],
                             bias=nmr[0:m, c:c + 1]).then_inc(h_act, 1)
            for c in range(NT):
                m = ROWS[c]
                if c >= 1:
                    high_part(2 * c)
                    high_part(2 * c + 1)
                act.wait_ge(hT_ps, c + 1)
                if c >= 2:
                    act.wait_ge(self_ps, c - 1)
                a.copy(hT[c % 2][:, 0, :, 0:m],
                       psA[:, c % 2, :].rearrange("p (k m) -> p k m", k=KD)[:, :, 0:m]).then_inc(hT_a, 1)
            for q in range(NQ):
                act.wait_ge(A_ps, q + 1)
                if q == 0:
                    act.wait_ge(self_ps, NT)
                if q >= 1:
                    act.wait_ge(A_s, q)
                    act.wait_ge(AT_b, q)
                a.mul(A32[:, :, :], psA[:, :, HC:2 * HC], 1.0 / LO_SCALE).then_inc(A_lo_ev, 1)
                act.wait_ge(A_ev, q + 1)
                if q >= 2:
                    act.wait_ge(G_ps, q - 1)
                a.copy(AT_hi[:, q % 2, :, :], A32[:, :, :]).then_inc(AT_a, 1)
                if q % 2 == 0 and q >= 2:
                    ln1_act(q // 2 - 1)
                act.wait_ge(G_ps, q + 1)
                if q == 0:
                    act.wait_ge(h_bs, NT)
                    act.wait_ge(hT_ps, NT)
                if q % 2 == 0 and q >= 2:
                    act.wait_ge(W_ps, q // 2)
                h = q % 2
                a.copy(G_hi[:, :, :, h * HD:(h + 1) * HD],
                       psGk.rearrange("p k (d r) -> p k r d", r=R)).then_inc(G_a, 1)
                if q % 2 == 0 and q >= 2:
                    turn_act(q // 2 - 1)
            for u in range(U_REL, U_W1):
                high_part(u)
            ln1_act(NT - 1)
            turn_act(NT - 1)
            for u in range(U_W1, NU):
                high_part(u)
            i = 0
            for g0, n in FG:
                for f in range(KF):
                    act.wait_ge(U_ps, i + 1)
                    if i >= 2:
                        act.wait_ge(U_b, i - 1)
                    a.activation(u32[:, i % 2, 0:n], psA[:, i % NT, 0:n], ACT.Gelu,
                                 bias=bf1[:, f:f + 1]).then_inc(U_g, 1)
                    i += 1
            for c in range(NT):
                m, b = ROWS[c], c % 2
                act.wait_ge(ln2_n, c + 1)
                a.activation(t2buf[0:m, b, :], t2buf[0:m, b, :], ACT.Identity, scale=rs2[0:m, b:b + 1],
                             bias=nm2[0:m, b:b + 1]).then_inc(y_hat, 1)

        @block.vector
        def _(dve):
            v = nc.vector
            chain = [0]

            def link(ins):
                chain[0] += 1
                ins.then_inc(dchain, 1)
                dve.wait_ge(dchain, chain[0])

            v.memset(rawB[0:ETB, 0, :], 0)
            v.memset(rawB[0:ETB, 1, :], N - 1)
            v.memset(small[:, 0:45], 0.0)
            v.memset(rawB[0:ETB, 2:4, :], 0).then_inc(pads, 1)
            dve.wait_ge(edges_in, 16 * 12)
            for t, (raw, n) in enumerate(((rawA, P), (rawB, ETB))):
                T = TF[t]
                v.tensor_copy(T[0:n, 0, :], raw[0:n, 0, :])
                v.scalar_tensor_tensor(out=T[0:n, 1, :], in0=raw[0:n, 1, :], scalar=float(R), in1=raw[0:n, 2, :],
                                       op0=ALU.mult, op1=ALU.add)
                link(v.tensor_copy(w16[t][0:n, :], raw[0:n, 3, :].bitcast(F32)))
                link(v.tensor_copy(T[0:n, 2, :], w16[t][0:n, :]))
                link(v.tensor_tensor(T[0:n, 3, :], raw[0:n, 3, :].bitcast(F32), T[0:n, 2, :], ALU.subtract))
                v.tensor_scalar(T[0:n, 3, :], T[0:n, 3, :], LO_SCALE, None, ALU.mult).then_inc(efields, 1)
                v.tensor_reduce(dmin[0:n, t:t + 1], raw[0:n, 1, :], AX.X, ALU.min)
                link(v.tensor_reduce(dmax[0:n, t:t + 1], raw[0:n, 1, :], AX.X, ALU.max))
            dve.wait_ge(iotas, 1)
            for t, n in ((0, P), (1, ETB)):
                v.tensor_scalar(dminm[0:n, t:t + 1], dmin[0:n, t:t + 1], float(-BW), None, ALU.add)
                v.tensor_scalar(ind[0:n, t, :], iota_blk[0:n, :], dmax[0:n, t:t + 1], None, ALU.is_gt).then_inc(find, 1)
            for c in range(NT):
                m = ROWS[c]
                dve.wait_ge(x_in[c], 16)
                link(v.bn_stats(stats[0:m, c, :], h32[0:m, c, :]))
                v.bn_aggr(mv[0:m, c, :], stats[0:m, c, :]).then_inc(xstat, 1)
            dve.wait_ge(fcnt, 1)
            link(v.tensor_scalar(fcol[:, :], psX[:, 0:NB], float(ET - SL), None, ALU.min))
            for t, n in ((0, P), (1, ETB)):
                v.scalar_tensor_tensor(out=ov[0:n, t, :], in0=iota_blk[0:n, :], scalar=dminm[0:n, t:t + 1],
                                       in1=ind[0:n, t, :], op0=ALU.is_gt, op1=ALU.is_gt)
                link(v.tensor_scalar(uu[0:n, t, :], fcol[0:n, :], negt[0:n, t:t + 1], (SL - 1) / 2.0, ALU.add, ALU.add))
                link(v.tensor_tensor(u2[0:n, t, :], uu[0:n, t, :], uu[0:n, t, :], ALU.mult))
                link(v.scalar_tensor_tensor(out=vv[0:n, t, :], in0=u2[0:n, t, :], scalar=((SL - 1) / 2.0) ** 2 + 1.0,
                                            in1=ov[0:n, t, :], op0=ALU.is_gt, op1=ALU.mult))
                v.tensor_reduce(vsum[0:n, t:t + 1], vv[0:n, t, :], AX.X, ALU.add).then_inc(viol, 1)
            v.tensor_copy(f_i32[:, 0:NB], fcol[:, :])
            dve.wait_ge(xrstd, 1)
            v.scalar_tensor_tensor(out=nmr, in0=mv[:, :, 0], scalar=-1.0, in1=rstd, op0=ALU.mult,
                                   op1=ALU.mult).then_inc(xnmr, 1)
            dve.wait_ge(eT, 1)
            v.tensor_copy(fields[:, :, 0:P], psG[:, 0, :].rearrange("p (f t) -> p f t", f=4))
            link(v.tensor_copy(fields[:, :, P:ET], psG[:, 1, 0:4 * P].rearrange("p (f t) -> p f t", f=4)[:, :, 0:ETB]))
            dve.wait_ge(vcnt, 1)
            v.tensor_copy(f_i32[:, NB:NB + 1], psX[:, 64:65]).then_inc(regs_in, 1)
            dve.wait_ge(regs_in, 1)
            flag = dve.value_load(f_i32[0:1, NB:NB + 1], min_val=0, max_val=1 << 20)

            def pick(b, first):
                v.tensor_tensor(slot[:, b % 2, :, :], fields[:, :, bass.ds(first, SL)],
                                key_off[:, b, :].unsqueeze(2).broadcast_to([P, 4, SL]), ALU.subtract).then_inc(gath, 1)

            def build(b):
                dve.wait_ge(gath, b + 1)
                if b >= 2:
                    dve.wait_ge(blk_used, b - 1)
                for j in range(SL):
                    s = (b % 2) * SL + j
                    v.tensor_scalar(onehot[:, s, :], iota_src[:, :], slot[:, b % 2, 0, j:j + 1], None, ALU.is_equal)
                    for part in range(2):
                        i = v.tensor_scalar(wkey[:, s, part * BC:(part + 1) * BC], iota_key[:, :],
                                            slot[:, b % 2, 1, j:j + 1], slot[:, b % 2, 2 + part, j:j + 1],
                                            ALU.is_equal, ALU.mult)
                i.then_inc(blk_in, 1)

            def firsts(q):
                return [dve.value_load(f_i32[0:1, HB * q + i:HB * q + i + 1], min_val=0, max_val=ET - SL)
                        for i in range(HB)]

            def evac_A(q):
                dve.wait_ge(A_lo_ev, q + 1)
                v.tensor_tensor(A32[:, :, :], psA[:, :, 0:HC], A32[:, :, :], ALU.add).then_inc(A_ev, 1)

            def evac_G(q):
                h = q % 2
                dve.wait_ge(G_a, q + 1)
                v.tensor_tensor(G_lo[:, :, :, h * HD:(h + 1) * HD], psGk.rearrange("p k (d r) -> p k r d", r=R),
                                f32(G_hi[:, :, :, h * HD:(h + 1) * HD]), ALU.subtract).then_inc(G_b, 1)

            def evac_D(q):
                h = q % 2
                dve.wait_ge(D_ps, q + 1)
                if q % 2 == 0 and q >= 2:
                    dve.wait_ge(W_ps, q // 2)
                v.tensor_tensor(dm[:, :], psX[0:R, 0:HC], mask_r[:, :], ALU.mult).then_inc(D_m, 1)
                dve.wait_ge(D_m, q + 1)
                v.tensor_reduce(D4[:, h * HD:(h + 1) * HD], dm[:, :].rearrange("k (d r) -> k d r", r=R),
                                AX.X, ALU.add).then_inc(D_ev, 1)

            def inv_deg(c):
                m = ROWS[c]
                dve.wait_ge(deg_ps, c + 1)
                v.tensor_scalar(rdeg[0:m, c:c + 1], psG[0:m, 0, 0:1], 1.0, None, ALU.max).then_inc(deg_m, 1)
                dve.wait_ge(deg_m, c + 1)
                v.reciprocal(rdeg[0:m, c:c + 1], rdeg[0:m, c:c + 1]).then_inc(deg_ev, 1)

            def ln1_a(c):
                m = ROWS[c]
                dve.wait_ge(W_ps, c + 1)
                dve.wait_ge(deg_ev, c + 1)
                if c >= 1:
                    dve.wait_ge(xhat_in, c)
                v.scalar_tensor_tensor(out=tbuf[0:m, :], in0=psX[0:m, :], scalar=rdeg[0:m, c:c + 1],
                                       in1=x1[0:m, c, :], op0=ALU.mult, op1=ALU.add).then_inc(t_out, 1)
                dve.wait_ge(t_out, 2 * c + 1)
                v.bn_stats(st1[0:m], tbuf[0:m, :]).then_inc(t_out, 1)
                dve.wait_ge(t_out, 2 * c + 2)
                v.bn_aggr(mv1[0:m], st1[0:m]).then_inc(ln1_v, 1)

            def ln1_b_(c):
                m = ROWS[c]
                dve.wait_ge(ln1_r, c + 1)
                v.scalar_tensor_tensor(out=nm1[0:m], in0=mv1[0:m, 0:1], scalar=-1.0, in1=rs1[0:m],
                                       op0=ALU.mult, op1=ALU.mult).then_inc(ln1_n, 1)

            def turn_low(c):
                m = ROWS[c]
                dve.wait_ge(xT_a, c + 1)
                v.tensor_tensor(x1T_lo[:, :, c * P:c * P + m],
                                psX[:, :].rearrange("p (k m) -> p k m", k=KD)[:, :, 0:m],
                                f32(x1T_hi[:, :, c * P:c * P + m]), ALU.subtract).then_inc(xT_b, 1)

            def general(q):
                with dve.If(flag > 0):
                    dve.wait_ge(blk_used, HB * (q + 1))
                    with dve.Fori(0, ET) as t:
                        v.tensor_copy(gslot[:, :], fields[:, :, bass.ds(t, 1)].squeeze(2)).then_inc(gen_m, 1)
                        dve.wait_ge(gen_m, t * 2 + (q * ET * 2 + 1))
                        v.tensor_scalar(gslot[:, 1:2], gslot[:, 1:2], float(q * HC), None, ALU.subtract).then_inc(gen_m, 1)
                        dve.wait_ge(gen_m, t * 2 + (q * ET * 2 + 2))
                        v.tensor_scalar(onehot[:, 0, :], iota_src[:, :], gslot[:, 0:1], None, ALU.is_equal)
                        for part in range(2):
                            i = v.tensor_scalar(gkey[:, part * HC:(part + 1) * HC], iota_src[:, 0:HC],
                                                gslot[:, 1:2], gslot[:, 2 + part:3 + part], ALU.is_equal, ALU.mult)
                        i.then_inc(gen_in, 1)
                        dve.wait_ge(gen_used, t + (q * ET + 1))

            r0 = firsts(0)
            for i in range(2):
                pick(i, r0[i])
                build(i)
            def self_low(c):
                m = ROWS[c]
                dve.wait_ge(hT_a, c + 1)
                v.tensor_tensor(hT[c % 2][:, 1, :, 0:m], psA[:, c % 2, :].rearrange("p (k m) -> p k m", k=KD)[:, :, 0:m],
                                f32(hT[c % 2][:, 0, :, 0:m]), ALU.subtract).then_inc(hT_b, 1)

            def self_add(c):
                m = ROWS[c]
                dve.wait_ge(self_ps, c + 1)
                dve.wait_ge(h_bs, c + 1)
                v.tensor_tensor(x1[0:m, c, :], psA[0:m, 2 + c % 2, :], x1[0:m, c, :], ALU.add).then_inc(self_ev, 1)

            for c in range(NT):
                self_low(c)
                if c >= 1:
                    self_add(c - 1)
            self_add(NT - 1)
            v.memset(f32(x1T_hi[:, :, N:NP]), 0.0).then_inc(self_ev, 1)
            v.memset(f32(x1T_lo[:, :, N:NP]), 0.0).then_inc(self_ev, 1)
            for i in range(2, HB):
                pick(i, r0[i])
                build(i)
            general(0)
            for q in range(NQ):
                more = q + 1 < NQ
                b = HB * (q + 1)
                if more:
                    r = firsts(q + 1)
                    pick(b, r[0])
                    build(b)
                evac_A(q)
                if more:
                    pick(b + 1, r[1])
                    build(b + 1)
                if q % 2 == 0 and q >= 2:
                    ln1_a(q // 2 - 1)
                if more:
                    pick(b + 2, r[2])
                    build(b + 2)
                if q % 2 == 0 and q >= 2:
                    ln1_b_(q // 2 - 1)
                if more:
                    pick(b + 3, r[3])
                    build(b + 3)
                    general(q + 1)
                evac_G(q)
                if q % 2 == 0 and q >= 2:
                    turn_low(q // 2 - 1)
                evac_D(q)
                if q % 2 == 1:
                    inv_deg(q // 2)
            ln1_a(NT - 1)
            ln1_b_(NT - 1)
            turn_low(NT - 1)
            i = 0
            for g0, n in FG:
                for f in range(KF):
                    dve.wait_ge(U_g, i + 1)
                    v.tensor_copy(u_hi[:, f, g0:g0 + n], u32[:, i % 2, 0:n]).then_inc(U_a, 1)
                    dve.wait_ge(U_a, i + 1)
                    v.tensor_tensor(u_lo[:, f, g0:g0 + n], u32[:, i % 2, 0:n], f32(u_hi[:, f, g0:g0 + n]),
                                    ALU.subtract).then_inc(U_b, 1)
                    i += 1
            for c in range(NT):
                m, b = ROWS[c], c % 2
                dve.wait_ge(Y_ps, c + 1)
                dve.wait_ge(x1b, c + 1)
                if c >= 2:
                    dve.wait_ge(y_out, c - 1)
                link(v.tensor_tensor(t2buf[0:m, b, :], ybank(c)[0:m], x1[0:m, c, :], ALU.add))
                link(v.bn_stats(st2[0:m, b, :], t2buf[0:m, b, :]))
                v.bn_aggr(mv2[0:m, b, :], st2[0:m, b, :]).then_inc(ln2_v, 1)
                dve.wait_ge(ln2_r, c + 1)
                v.scalar_tensor_tensor(out=nm2[0:m, b:b + 1], in0=mv2[0:m, b, 0:1], scalar=-1.0, in1=rs2[0:m, b:b + 1],
                                       op0=ALU.mult, op1=ALU.mult).then_inc(ln2_n, 1)

        @block.tensor
        def _(pe):
            def mm(o, l, r, start, stop=False):
                return nc.tensor.matmul(o, l, r, start=start, stop=stop, skip_group_check=True)

            pe.wait_ge(iotas, 1)
            pe.wait_ge(efields, 2)
            for t, n in ((0, P), (1, ETB)):
                for f in range(4):
                    i = nc.tensor.transpose(psG[:, t, f * P:f * P + n], TF[t][0:n, f, :], ident[0:n, 0:n])
            i.then_inc(eT, 1)
            pe.wait_ge(find, 2)
            mm(psX[:, 0:NB], ones[:, :], ind[:, 0, :], True)
            mm(psX[:, 0:NB], ones[0:ETB, :], ind[0:ETB, 1, :], False, True).then_inc(fcnt, 1)
            pe.wait_ge(viol, 2)
            mm(psX[:, 64:65], ones[:, :], vsum[:, 0:1], True)
            mm(psX[:, 64:65], ones[0:ETB, :], vsum[0:ETB, 1:2], False, True).then_inc(vcnt, 1)
            pe.wait_ge(h_act, 2)

            def turn_h(c):
                m = ROWS[c]
                pe.wait_ge(h_act, 2 * (c + 1))
                if c >= 2:
                    pe.wait_ge(hT_b, c - 1)
                for k in range(KD):
                    i = nc.tensor.transpose(psA[:, c % 2, k * P:k * P + m], h32[0:m, c, k * P:(k + 1) * P],
                                            ident[0:m, 0:m])
                i.then_inc(hT_ps, 1)

            def self_product(c):
                m = ROWS[c]
                pe.wait_ge(hT_b, c + 1)
                pe.wait_ge(w_lo, U_SELF)
                if c >= 2:
                    pe.wait_ge(self_ev, c - 1)
                t, o = hT[c % 2], psA[0:m, 2 + c % 2, :]
                for k in range(KD):
                    mm(o, t[:, 0, k, 0:m], wself_hi[:, k, :], k == 0)
                    mm(o, t[:, 1, k, 0:m], wself_hi[:, k, :], False)
                    i = mm(o, t[:, 0, k, 0:m], wself_lo[:, k, :], False, k == KD - 1)
                i.then_inc(self_ps, 1)

            def build(q, blocks):
                for i in blocks:
                    b = HB * q + i
                    pe.wait_ge(blk_in, b + 1)
                    for j in range(SL):
                        s = (b % 2) * SL + j
                        for t in range(NT):
                            o = psA[:, t, :].rearrange("p (h n) -> p h n", h=2)[:, :, i * BC:(i + 1) * BC]
                            last = mm(o, onehot[:, s, t * P:(t + 1) * P], wkey[:, s, :],
                                      i == 0 and j == 0, i == HB - 1 and j == SL - 1)
                    last.then_inc(blk_used, 1)

            def finish_A(q):
                with pe.If(flag > 0):
                    pe.wait_ge(gen_in, q * ET + 1)
                    general_tile(True).then_inc(gen_used, 1)
                    with pe.Fori(1, ET) as t:
                        pe.wait_ge(gen_in, t + (q * ET + 1))
                        general_tile(False).then_inc(gen_used, 1)
                mm(psA[0:64, NT - 1, 0:2], zeros[:, :], zeros[:, 0:2], False, True).then_inc(A_ps, 1)

            def general_tile(start):
                for t in range(NT):
                    i = mm(psA[:, t, :], onehot[:, 0, t * P:(t + 1) * P], gkey, start)
                return i

            def G_part(q, ks):
                pe.wait_ge(AT_a, q + 1)
                pe.wait_ge(AT_b, q + 1)
                b = q % 2
                for k in ks:
                    o = psGk[:, k, :]
                    for s in range(NT):
                        m = ROWS[s]
                        hh, hl = (h_hi[0:m, s, k * P:(k + 1) * P], h_lo[0:m, s, k * P:(k + 1) * P])
                        mm(o, hh, AT_hi[0:m, b, s, :], k % 2 == 0 and s == 0)
                        mm(o, hl, AT_hi[0:m, b, s, :], False)
                        last = mm(o, hh, AT_lo[0:m, b, s, :], False, s == NT - 1)
                return last

            def degrees(q):
                pe.wait_ge(A_s, q + 1)
                if q >= 1:
                    pe.wait_ge(D_ev, q)
                mm(psX[:, 0:HC], ones[:, :], A_sum[:, :], True, True).then_inc(D_ps, 1)

            def turn_x1(c):
                m = ROWS[c]
                pe.wait_ge(x1_in, c + 1)
                for k in range(KD):
                    i = nc.tensor.transpose(psX[:, k * P:k * P + m], x1[0:m, c, k * P:(k + 1) * P], ident[0:m, 0:m])
                i.then_inc(xT_ps, 1)

            def rel_product(c):
                m = ROWS[c]
                pe.wait_ge(D_ev, 2 * c + 2)
                pe.wait_ge(G_b, 2 * c + 2)
                mm(psG[0:m, 0, 0:1], D4[:, 0:m], ones[0:R, 0:1], True, True).then_inc(deg_ps, 1)
                mm(psX[0:m, :], D4[:, 0:m], brel_sb[:, :], True)
                for r in range(R):
                    if c == 0:
                        pe.wait_ge(w_lo, U_SELF + 2 * (r + 1))
                    for k in range(KD):
                        mm(psX[0:m, :], G_hi[:, k, r, 0:m], wrel_hi[:, r, k, :], False)
                        mm(psX[0:m, :], G_lo[:, k, r, 0:m], wrel_hi[:, r, k, :], False)
                        i = mm(psX[0:m, :], G_hi[:, k, r, 0:m], wrel_lo[:, r, k, :], False,
                               r == R - 1 and k == KD - 1)
                i.then_inc(W_ps, 1)

            for c in range(NT):
                turn_h(c)
                if c >= 1:
                    self_product(c - 1)
            self_product(NT - 1)
            pe.wait_ge(self_ev, NT)
            pe.wait_ge(h_los, NT)
            pe.wait_ge(regs_in, 1)
            flag = pe.value_load(f_i32[0:1, NB:NB + 1], min_val=0, max_val=1 << 20)
            build(0, range(HB))
            finish_A(0)
            for q in range(NQ):
                if q + 1 < NQ:
                    pe.wait_ge(A_ev, q + 1)
                    build(q + 1, range(0, 2))
                if q >= 1:
                    pe.wait_ge(G_b, q)
                if q >= 2 and q % 2 == 0:
                    pe.wait_ge(deg_ev, q // 2)
                if q % 2 == 0:
                    G_part(q, range(0, KD - 1))
                    if q >= 2:
                        turn_x1(q // 2 - 1)
                    build(q + 1, range(2, 4))
                    finish_A(q + 1)
                    G_part(q, range(KD - 1, KD)).then_inc(G_ps, 1)
                    if q >= 2:
                        pe.wait_ge(xT_b, q // 2)
                    degrees(q)
                else:
                    G_part(q, range(KD)).then_inc(G_ps, 1)
                    degrees(q)
                    if q + 1 < NQ:
                        build(q + 1, range(2, 4))
                        finish_A(q + 1)
                    rel_product(q // 2)
            i = 0
            for g, (g0, n) in enumerate(FG):
                if g == 1:
                    pe.wait_ge(xT_b, NT)
                for f in range(KF):
                    if i == 0:
                        pe.wait_ge(w_lo, U_W1)
                    if i == NT:
                        turn_x1(NT - 1)
                    if i >= NT:
                        pe.wait_ge(U_g, i - NT + 1)
                    o = psA[:, i % NT, 0:n]
                    for k in range(KD):
                        wh, wl = W1_hi[:, k, f * P:(f + 1) * P], W1_lo[:, k, f * P:(f + 1) * P]
                        mm(o, wh, x1T_hi[:, k, g0:g0 + n], k == 0)
                        mm(o, wh, x1T_lo[:, k, g0:g0 + n], False)
                        last = mm(o, wl, x1T_hi[:, k, g0:g0 + n], False, k == KD - 1)
                    last.then_inc(U_ps, 1)
                    i += 1
            pe.wait_ge(w_lo, NU)
            for c in range(NT):
                m = ROWS[c]
                pe.wait_ge(U_b, KF if c < 3 else 2 * KF)
                if c >= 3:
                    pe.wait_ge(ln2_v, c - 2)
                o = ybank(c)[0:m]
                for f in range(KF):
                    uh, ul = u_hi[:, f, c * P:c * P + m], u_lo[:, f, c * P:c * P + m]
                    mm(o, uh, W2_hi[:, f, :], f == 0)
                    mm(o, ul, W2_hi[:, f, :], False)
                    last = mm(o, uh, W2_lo[:, f, :], False, f == KF - 1)
                last.then_inc(Y_ps, 1)


_INS = ["x", "src", "dst", "edge_type_4", "edge_weight", "L0_gnn_W_self", "L0_gnn_b_self", "L0_gnn_W_rel",
        "L0_gnn_b_rel", "L0_gnn_ln1_g", "L0_gnn_ln1_b", "L0_gnn_ln2_g", "L0_gnn_ln2_b", "L0_gnn_W_ffn1",
        "L0_gnn_b_ffn1", "L0_gnn_W_ffn2", "L0_gnn_b_ffn2"]


def kernel(**inputs):
    import numpy as np
    import concourse.bacc as bacc
    from concourse.bass_utils import run_bass_kernel_spmd as run

    nc = bacc.Bacc("TRN2", target_bir_lowering=False, num_devices=1)
    arrays, args = {}, []
    for name in _INS:
        a = np.ascontiguousarray(inputs[name])
        arrays[f"in_{name}"] = a
        args.append(nc.dram_tensor(f"in_{name}", a.shape, mybir.dt.from_np(a.dtype), kind="ExternalInput").ap())
    shape = inputs["x"].shape
    args.append(nc.dram_tensor("out_0", shape, F32, kind="ExternalOutput").ap())
    gnn_layer(nc, *args)
    r = run(nc, [arrays], core_ids=[0])
    return r.results[0]["out_0"]
```

```python
from contextlib import ExitStack

import concourse.bass as bass
from concourse import mybir


F32 = mybir.dt.float32
F32R = mybir.dt.float32r
F16 = mybir.dt.float16
I32 = mybir.dt.int32
ALU = mybir.AluOpType
ACT = mybir.ActivationFunctionType
AX = mybir.AxisListType

P = 128
LO_SCALE = 4096.0
EPS = 1e-5


def gnn_layer(nc, x, src, dst, etype, ew, W_self, b_self, W_rel, b_rel, ln1_g, ln1_b, ln2_g, ln2_b,
              W1, b1, W2, b2, out):
    N, D = x.shape
    E = src.shape[0]
    R = W_rel.shape[0]
    F = W1.shape[1]
    KD = D // P
    KF = F // P
    NT = -(-N // P)
    NP = NT * P
    ROWS = [min(P, N - c * P) for c in range(NT)]
    EK = N // 5
    ET = E // EK
    EG = 3
    EP = ET // EG
    BW = 16
    BC = BW * R
    NB = NP // BW
    HB = 4
    HC = HB * BC
    HD = HB * BW
    NQ = NB // HB
    SL = 6
    RING = 2 * SL
    assert EK * ET == E and EG * EP == ET and R * EK <= 512
    UC = 1024
    FG = [(0, 3 * P), (3 * P, NP - 3 * P)]

    base = nc.sbuf_base + (-nc.sbuf_base) % 64

    def sb(name, shape, dt, kb):
        return nc.alloc_sbuf_tensor_at(name, shape, dt, offset=base + int(kb * 1024))

    wrel_hi = sb("wrel_hi", [P, R, KD, D], F32R, 0)
    wrel_lo = sb("wrel_lo", [P, R, KD, D], F32R, 32)
    wself_hi = sb("wself_hi", [P, KD, D], F32R, 64)
    wself_lo = sb("wself_lo", [P, KD, D], F32R, 72)
    x1T_hi = sb("x1T_hi", [P, KD, NP], F32R, 64)
    x1T_lo = sb("x1T_lo", [P, KD, NP], F32R, 74)
    onehot = sb("onehot", [P, RING, NP], F16, 84)
    wkey = sb("wkey", [P, RING, 2 * BC], F16, 99)
    keq = sb("keq", [P, SL, BC], F16, 202.25)
    AT_hi = sb("AT_hi", [P, 2, NT, HC], F32R, 102)
    AT_lo = sb("AT_lo", [P, 2, NT, HC], F32R, 112)
    A32 = sb("A32", [P, NT, HC], F32, 122)
    G_hi = sb("G_hi", [P, KD, R, P], F32R, 127)
    G_lo = sb("G_lo", [P, KD, R, P], F32R, 135)
    h32 = sb("h32", [P, NT, D], F32, 127)
    hT = [sb("hT0", [P, 2, KD, P], F32R, 122), sb("hT1", [P, 2, KD, P], F32R, 137)]
    h_hi = sb("h_hi", [P, NT, D], F32R, 143)
    h_lo = sb("h_lo", [P, NT, D], F32R, 153)
    x1 = sb("x1", [P, NT, D], F32, 163)
    bself_bc = sb("bself_bc", [P, D], F32, 173)
    g1_bc = sb("g1_bc", [P, D], F32, 175)
    b1_bc = sb("b1_bc", [P, D], F32, 177)
    stage = sb("stage", [P, 3, UC], F32, 179)
    fields = sb("fields", [P, 4, ET], F32, 191)
    iota_src = sb("iota_src", [P, NP], F16, 193.75)
    iota_key = sb("iota_key", [P, BC], F16, 195)
    zeros = sb("zeros", [P, 64], F16, 195.125)
    ident = sb("ident", [P, P], F32, 195.25)
    ones = sb("ones", [P, P], F32, 195.75)
    key_off = sb("key_off", [P, NB, 4], F32, 196.25)
    slot = sb("slot", [P, 2, 4, SL], F32, 197)
    A_sum = sb("A_sum", [P, HC], F32, 197.25)
    brel_sb = sb("brel_sb", [R, D], F32, 198.25)
    tbuf = sb("tbuf", [P, D], F32, 200.25)
    D4 = sb("D4", [R, P], F32, 204.25)
    small = sb("small", [P, 160], F32, 204.75)
    mask_r = sb("mask_r", [R, HC], F32, 205.5)
    f_i32 = sb("f_i32", [P, NB + 8], I32, 206.5)
    dm = sb("dm", [R, HC], F32, 206.75)
    gkey = wkey[:, 0:4, :].rearrange("p s n -> p (s n)")
    raw = sb("raw", [EP, 4, EG * EK], I32, 102)
    TF = sb("TF", [EP, 4, EG * EK], F32, 108)
    w16 = sb("w16", [EP, EG * EK], F16, 114)
    iota_blk = sb("iota_blk", [P, NB], F32, 115)
    ind = sb("ind", [EP, EG, NB], F32, 115.25)
    ov = sb("ov", [EP, EG, NB], F32, 116)
    uu = sb("uu", [EP, EG, NB], F32, 116.5)
    u2 = sb("u2", [EP, EG, NB], F32, 117)
    vv = sb("vv", [EP, EG, NB], F32, 117.5)
    fcol = sb("fcol", [P, NB], F32, 118)
    W1_hi = sb("W1_hi", [P, KD, F], F32R, 84)
    W1_lo = sb("W1_lo", [P, KD, F], F32R, 102)
    W2_hi = sb("W2_hi", [P, KF, D], F32R, 143)
    W2_lo = sb("W2_lo", [P, KF, D], F32R, 127)
    u_hi = sb("u_hi", [P, KF, NP], F32R, 0)
    u_lo = sb("u_lo", [P, KF, NP], F32R, 20)
    u32 = sb("u32", [P, 2, 3 * P], F32, 40)
    x_again = sb("x_again", [P, NT, D], F32, 44)
    g2_bc = sb("g2_bc", [P, D], F32, 54)
    b2_bc = sb("b2_bc", [P, D], F32, 56)
    bf2_bc = sb("bf2_bc", [P, D], F32, 58)
    ybuf = sb("ybuf", [P, 2, D], F32, 60)
    t2buf = sb("t2buf", [P, 2, D], F32, 122)

    stats = small[:, 0:30].rearrange("p (c s) -> p c s", s=6)
    mv = small[:, 30:40].rearrange("p (c s) -> p c s", s=2)
    rstd = small[:, 40:45]
    nmr = small[:, 45:50]
    mhalf = small[:, 50:55]
    var_e = small[:, 55:60]
    rdeg = small[:, 60:65]
    dmin = small[0:EP, 65:65 + EG]
    dmax = small[0:EP, 68:68 + EG]
    dminm = small[0:EP, 71:71 + EG]
    negt = small[0:EP, 132:132 + EG]
    vsum = small[0:EP, 135:136]
    bf1 = small[:, 76:76 + KF]
    st1 = small[:, 84:90]
    mv1 = small[:, 90:92]
    ve1 = small[:, 92:93]
    rs1 = small[:, 93:94]
    nm1 = small[:, 94:95]
    st2 = small[:, 100:112].rearrange("p (c s) -> p c s", s=6)
    mv2 = small[:, 112:116].rearrange("p (c s) -> p c s", s=2)
    ve2 = small[:, 116:118]
    rs2 = small[:, 118:120]
    nm2 = small[:, 120:122]

    gslot = small[:, 124:128]

    psA = nc.alloc_psum_tensor("psA", [P, NT, 512], F32)
    psG = nc.alloc_psum_tensor("psG", [P, 2, 512], F32)
    psX = nc.alloc_psum_tensor("psX", [P, 512], F32)
    psGk = psG[:, :, :].rearrange("p b (k n) -> p (b k) n", k=2)

    ctx = ExitStack()
    with ctx:
        def sem(name):
            return ctx.enter_context(nc.semaphore(name))

        dst_in = sem("dst_in")
        edges_in = sem("edges_in")
        x_in = [sem(f"x_in{c}") for c in range(NT)]
        consts_in = sem("consts_in")
        stage_in = [sem(f"stage_in{i}") for i in range(3)]
        late_in = sem("late_in")
        out_done = [sem(f"out_done{i}") for i in range(2)]
        iotas = sem("iotas")
        dchain = sem("dchain")
        pchain = sem("pchain")
        w_high_in = sem("w_high_in")
        efields = sem("efields")
        srcs = sem("srcs")
        first_in = sem("first_in")
        eT = sem("eT")
        find = sem("find")
        fcnt = sem("fcnt")
        viol = sem("viol")
        vcnt = sem("vcnt")
        regs_in = sem("regs_in")
        xstat = sem("xstat")
        xrstd = sem("xrstd")
        xnmr = sem("xnmr")
        h_act = sem("h_act")
        h_los = sem("h_los")
        h_bs = sem("h_bs")
        w_hi = sem("w_hi")
        w_lo = sem("w_lo")
        w1_lo = sem("w1_lo")
        hT_ps = sem("hT_ps")
        hT_a = sem("hT_a")
        hT_b = sem("hT_b")
        self_ps = sem("self_ps")
        turned = sem("turned")
        xpad = sem("xpad")
        self_ev = sem("self_ev")
        gath = sem("gath")
        keq_in = sem("keq_in")
        blk_in = sem("blk_in")
        blk_used = sem("blk_used")
        gen_in = sem("gen_in")
        gen_m = sem("gen_m")
        gen_used = sem("gen_used")
        A_ps = sem("A_ps")
        A_lo_ev = sem("A_lo_ev")
        A_ev = sem("A_ev")
        AT_a = sem("AT_a")
        AT_b = sem("AT_b")
        A_s = sem("A_s")
        G_ps = sem("G_ps")
        G_a = sem("G_a")
        G_b = sem("G_b")
        D_ps = sem("D_ps")
        D_m = sem("D_m")
        D_ev = sem("D_ev")
        deg_ps = sem("deg_ps")
        deg_m = sem("deg_m")
        deg_ev = sem("deg_ev")
        W_ps = sem("W_ps")
        t_out = sem("t_out")
        ln1_s = sem("ln1_s")
        ln1_v = sem("ln1_v")
        ln1_r = sem("ln1_r")
        ln1_n = sem("ln1_n")
        xhat_in = sem("xhat_in")
        x1_in = sem("x1_in")
        xT_ps = sem("xT_ps")
        xT_a = sem("xT_a")
        xT_b = sem("xT_b")
        U_ps = sem("U_ps")
        U_g = sem("U_g")
        U_a = sem("U_a")
        U_b = sem("U_b")
        x1b = sem("x1b")
        Y_ps = sem("Y_ps")
        Y_ev = sem("Y_ev")
        ln2_v = sem("ln2_v")
        ln2_r = sem("ln2_r")
        ln2_n = sem("ln2_n")
        y_hat = sem("y_hat")
        y_g = sem("y_g")
        y_out = sem("y_out")

        block = ctx.enter_context(nc.Block())

        units = []
        for k in range(0, KD, 2):
            units.append((W_self.rearrange("(k p) n -> p k n", p=P)[:, k:k + 2, :],
                          wself_hi[:, k:k + 2, :], wself_lo[:, k:k + 2, :]))
        for r in range(R):
            for k in range(0, KD, 2):
                units.append((W_rel[r].rearrange("(k p) n -> p k n", p=P)[:, k:k + 2, :],
                              wrel_hi[:, r, k:k + 2, :], wrel_lo[:, r, k:k + 2, :]))
        U_SELF, U_REL = 2, 2 + 2 * R
        for k in range(KD):
            units.append((W1[k * P:(k + 1) * P, :], W1_hi[:, k, :], W1_lo[:, k, :]))
        U_W1 = U_REL + KD
        for k in range(0, KF, 2):
            units.append((W2.rearrange("(k p) n -> p k n", p=P)[:, k:k + 2, :],
                          W2_hi[:, k:k + 2, :], W2_lo[:, k:k + 2, :]))
        NU = len(units)

        def stage_view(u):
            v = stage[:, u % 3, :]
            return v if U_REL <= u < U_W1 else v.rearrange("p (k n) -> p k n", k=2)

        def split(u):
            if u < U_REL:
                return w_lo, u + 1
            return (w1_lo, u - U_REL + 1) if u < U_W1 else (w_lo, u + 1 - KD)

        def f32(ap):
            return ap.bitcast(F32)

        def self_bank(c):
            return [psX[:, :], psG[:, 1, :]][c % 2]

        def ybank(c):
            return [psG[:, 0, :], psG[:, 1, :], psX[:, :]][c % 3]

        def low_part(eng, u):
            eng.wait_ge(w_hi, u + 1)
            done = split(u)[0]
            eng.tensor_tensor(units[u][2], stage_view(u), f32(units[u][1]), ALU.subtract).then_inc(done, 1)

        def ln1_pool(c):
            g, pool, m = nc.gpsimd, nc.gpsimd, ROWS[c]
            pool.wait_ge(ln1_v, c + 1)
            g.tensor_scalar(ve1[0:m], mv1[0:m, 1:2], EPS, None, ALU.add).then_inc(ln1_s, 1)
            pool.wait_ge(ln1_s, 2 * c + 1)
            g.tensor_tensor(rs1[0:m], ve1[0:m], mhalf[0:m, 0:1], ALU.pow).then_inc(ln1_r, 1)
            pool.wait_ge(xhat_in, c + 1)
            g.tensor_tensor(tbuf[0:m, :], tbuf[0:m, :], g1_bc[0:m, :], ALU.mult).then_inc(ln1_s, 1)
            pool.wait_ge(ln1_s, 2 * c + 2)
            g.tensor_tensor(x1[0:m, c, :], tbuf[0:m, :], b1_bc[0:m, :], ALU.add).then_inc(x1_in, 1)

        def ln1_act(c):
            a, m = nc.scalar, ROWS[c]
            a.wait_ge(ln1_n, c + 1)
            a.activation(tbuf[0:m, :], tbuf[0:m, :], ACT.Identity, scale=rs1[0:m], bias=nm1[0:m]).then_inc(xhat_in, 1)

        def turn_act(c):
            a, m = nc.scalar, ROWS[c]
            a.wait_ge(xT_ps, c + 1)
            a.copy(x1T_hi[:, :, c * P:c * P + m],
                   psX[:, :].rearrange("p (k m) -> p k m", k=KD)[:, :, 0:m]).then_inc(xT_a, 1)

        @block.sync
        def _(sp):
            sp.dma_start(raw[:, 1, :], dst.rearrange("(p e) -> p e", p=EP)).then_inc(dst_in, 16)
            sp.dma_start(raw[:, 2, :], etype.rearrange("(p e) -> p e", p=EP)).then_inc(edges_in, 16)
            for c in range(NT):
                sp.dma_start(h32[0:ROWS[c], c, :], x[c * P:c * P + ROWS[c], :]).then_inc(x_in[c], 16)
                if c == 0:
                    for u in range(3):
                        sp.dma_start(stage_view(u), units[u][0]).then_inc(stage_in[u % 3], 16)
            for u in range(3, NU):
                sp.wait_ge(*split(u - 3))
                sp.dma_start(stage_view(u), units[u][0]).then_inc(stage_in[u % 3], 16)
            sp.wait_ge(W_ps, NT)
            for c in range(NT):
                sp.dma_start(x_again[0:ROWS[c], c, :], x[c * P:c * P + ROWS[c], :]).then_inc(late_in, 16)
            for buf, v in ((g2_bc, ln2_g), (b2_bc, ln2_b), (bf2_bc, b2)):
                sp.dma_start(buf[:, :], v.rearrange("(a d) -> a d", a=1).broadcast_to([P, D])).then_inc(late_in, 16)
            for c in range(NT):
                sp.wait_ge(y_out, c + 1)
                sp.dma_start(out[c * P:c * P + ROWS[c], :], ybuf[0:ROWS[c], c % 2, :]).then_inc(out_done[c % 2], 16)
            for i in range(2):
                sp.wait_ge(out_done[i], 16 * len(range(i, NT, 2)))

        @block.gpsimd
        def _(pool):
            chain = [0]

            def link(ins):
                chain[0] += 1
                ins.then_inc(pchain, 1)
                pool.wait_ge(pchain, chain[0])

            g = nc.gpsimd
            g.iota(iota_src[:, :], [[1, NP]], base=0, channel_multiplier=0, allow_small_or_imprecise_dtypes=True)
            g.iota(iota_key[:, :], [[1, BC]], base=0, channel_multiplier=0, allow_small_or_imprecise_dtypes=True)
            g.iota(iota_blk[:, :], [[BW, NB]], base=0, channel_multiplier=0, allow_small_or_imprecise_dtypes=True)
            g.iota(negt, [[-1, EG]], base=0, channel_multiplier=-EG, allow_small_or_imprecise_dtypes=True)
            g.memset(ones[:, :], 1.0)
            link(g.memset(key_off[:, :, :], 0.0))
            g.iota(key_off[:, :, 1], [[BC, NB]], base=0, channel_multiplier=0, allow_small_or_imprecise_dtypes=True)
            g.memset(mhalf, -0.5)
            link(g.memset(ident[:, :], 0.0))
            g.affine_select(out=ident[:, :], in_=ident[:, :], compare_op=ALU.not_equal, fill=1.0, base=0,
                            pattern=[[-1, P]], channel_multiplier=1)
            link(g.memset(mask_r[:, :], 0.0))
            link(g.affine_select(out=mask_r[:, :].rearrange("k (d r) -> k d r", r=R),
                                 in_=mask_r[:, :].rearrange("k (d r) -> k d r", r=R),
                                 compare_op=ALU.not_equal, fill=1.0, base=0,
                                 pattern=[[0, HD], [-1, R]], channel_multiplier=1))
            g.memset(zeros[:, :], 0.0).then_inc(iotas, 1)
            pool.wait_ge(xstat, NT)
            link(g.tensor_scalar(var_e, mv[:, :, 1], EPS, None, ALU.add))
            g.tensor_tensor(rstd, var_e, mhalf, ALU.pow).then_inc(xrstd, 1)
            for u in range(U_SELF):
                low_part(pool, u)
            pool.wait_ge(consts_in, 16 * 5)
            for c in range(NT):
                m = ROWS[c]
                pool.wait_ge(h_act, 2 * (c + 1))
                g.tensor_tensor(x1[0:m, c, :], h32[0:m, c, :], bself_bc[0:m, :], ALU.add).then_inc(h_bs, 1)
                g.tensor_tensor(h_lo[0:m, c, :], h32[0:m, c, :], f32(h_hi[0:m, c, :]), ALU.subtract).then_inc(h_los, 1)
            for u in range(U_SELF, U_REL):
                low_part(pool, u)
            for q in range(NQ):
                pool.wait_ge(A_ev, q + 1)
                if q >= 1:
                    pool.wait_ge(D_ps, q)
                link(g.tensor_tensor(A_sum[:, :], A32[:, 0, :], A32[:, 1, :], ALU.add))
                for s in range(2, NT):
                    i = g.tensor_tensor(A_sum[:, :], A_sum[:, :], A32[:, s, :], ALU.add)
                    if s < NT - 1:
                        link(i)
                i.then_inc(A_s, 1)
                if q % 2 == 0 and q >= 2:
                    ln1_pool(q // 2 - 1)
            ln1_pool(NT - 1)
            pool.wait_ge(W_ps, NT)
            for u in range(U_W1, NU):
                low_part(pool, u)
            pool.wait_ge(late_in, 16 * (NT + 3))
            for c in range(NT):
                m = ROWS[c]
                pool.wait_ge(xT_ps, c + 1)
                g.tensor_tensor(x_again[0:m, c, :], x_again[0:m, c, :], b2_bc[0:m, :], ALU.add)
                g.tensor_tensor(x1[0:m, c, :], x1[0:m, c, :], bf2_bc[0:m, :], ALU.add).then_inc(x1b, 1)
            for c in range(NT):
                m, b = ROWS[c], c % 2
                pool.wait_ge(ln2_v, c + 1)
                link(g.tensor_scalar(ve2[0:m, b:b + 1], mv2[0:m, b, 1:2], EPS, None, ALU.add))
                g.tensor_tensor(rs2[0:m, b:b + 1], ve2[0:m, b:b + 1], mhalf[0:m, 0:1], ALU.pow).then_inc(ln2_r, 1)

        @block.scalar
        def _(act):
            a = nc.scalar
            act.dma_start(raw[:, 3, :], ew.bitcast(I32).rearrange("(p e) -> p e", p=EP)).then_inc(edges_in, 16)
            act.dma_start(raw[:, 0, :], src.rearrange("(p e) -> p e", p=EP)).then_inc(edges_in, 16)
            for buf, v in ((bself_bc, b_self), (g1_bc, ln1_g), (b1_bc, ln1_b)):
                act.dma_start(buf[:, :], v.rearrange("(a d) -> a d", a=1).broadcast_to([P, D])).then_inc(consts_in, 16)
            act.dma_start(brel_sb[:, :], b_rel).then_inc(consts_in, 16)
            with nc.allow_non_contiguous_dma("bias by partition"):
                act.dma_start(bf1, b1.rearrange("(f p) -> p f", p=P)).then_inc(consts_in, 16)

            def high_part(u):
                act.wait_ge(stage_in[u % 3], 16 * (u // 3 + 1))
                if u == U_REL:
                    act.wait_ge(blk_used, NB)
                if u == U_W1:
                    act.wait_ge(G_ps, NQ)
                a.copy(units[u][1], stage_view(u)).then_inc(w_hi, 1)

            act.wait_ge(edges_in, 16 * 3)
            a.copy(w16[:, :], raw[:, 3, :].bitcast(F32)).then_inc(w_high_in, 1)
            act.wait_ge(w_high_in, 1)
            a.copy(TF[:, 2, :], w16[:, :]).then_inc(w_high_in, 1)
            a.copy(TF[:, 0, :], raw[:, 0, :]).then_inc(srcs, 1)
            high_part(0)
            high_part(1)
            act.wait_ge(xnmr, 1)
            for c in range(NT):
                m = ROWS[c]
                a.activation(h_hi[0:m, c, :], h32[0:m, c, :], ACT.Relu, scale=rstd[0:m, c:c + 1],
                             bias=nmr[0:m, c:c + 1]).then_inc(h_act, 1)
                act.wait_ge(h_act, 2 * c + 1)
                a.activation(h32[0:m, c, :], h32[0:m, c, :], ACT.Relu, scale=rstd[0:m, c:c + 1],
                             bias=nmr[0:m, c:c + 1]).then_inc(h_act, 1)
            for c in range(NT):
                m = ROWS[c]
                if c >= 1:
                    high_part(2 * c)
                    high_part(2 * c + 1)
                act.wait_ge(hT_ps, c + 1)
                if c >= 2:
                    act.wait_ge(self_ps, c - 1)
                a.copy(hT[c % 2][:, 0, :, 0:m],
                       psG[:, 0, :].rearrange("p (k m) -> p k m", k=KD)[:, :, 0:m]).then_inc(hT_a, 1)

            def A_low_weights(q):
                act.wait_ge(A_ps, q + 1)
                if q == 0:
                    act.wait_ge(self_ps, NT)
                if q >= 1:
                    act.wait_ge(A_s, q)
                    act.wait_ge(AT_b, q)
                a.mul(A32[:, :, :], psA[:, :, HC:2 * HC], 1.0 / LO_SCALE).then_inc(A_lo_ev, 1)

            def A_high(q):
                act.wait_ge(A_ev, q + 1)
                if q >= 2:
                    act.wait_ge(G_ps, q - 1)
                a.copy(AT_hi[:, q % 2, :, :], A32[:, :, :]).then_inc(AT_a, 1)

            def G_high(q):
                act.wait_ge(G_ps, q + 1)
                if q == 0:
                    act.wait_ge(h_bs, NT)
                    act.wait_ge(h_los, NT)
                    act.wait_ge(hT_ps, NT)
                if q % 2 == 0 and q >= 2:
                    act.wait_ge(W_ps, q // 2)
                h = q % 2
                a.copy(G_hi[:, :, :, h * HD:(h + 1) * HD],
                       psGk.rearrange("p k (d r) -> p k r d", r=R)).then_inc(G_a, 1)

            A_low_weights(0)
            A_high(0)
            for q in range(NQ):
                if q % 2 == 0:
                    if q >= 2:
                        ln1_act(q // 2 - 1)
                        turn_act(q // 2 - 1)
                    A_low_weights(q + 1)
                    G_high(q)
                    A_high(q + 1)
                else:
                    G_high(q)
                    if q + 1 < NQ:
                        A_low_weights(q + 1)
                        A_high(q + 1)
            for u in range(U_REL, U_W1):
                high_part(u)
            ln1_act(NT - 1)
            turn_act(NT - 1)
            for u in range(U_W1, NU):
                high_part(u)
            i = 0
            for g0, n in FG:
                for f in range(KF):
                    act.wait_ge(U_ps, i + 1)
                    if i >= 2:
                        act.wait_ge(U_b, i - 1)
                    a.activation(u32[:, i % 2, 0:n], psA[:, i % NT, 0:n], ACT.Gelu,
                                 bias=bf1[:, f:f + 1]).then_inc(U_g, 1)
                    i += 1
            for c in range(NT):
                m, b = ROWS[c], c % 2
                act.wait_ge(ln2_n, c + 1)
                a.activation(t2buf[0:m, b, :], t2buf[0:m, b, :], ACT.Identity, scale=rs2[0:m, b:b + 1],
                             bias=nm2[0:m, b:b + 1]).then_inc(y_hat, 1)

        @block.vector
        def _(dve):
            v = nc.vector
            chain = [0]

            def link(ins):
                chain[0] += 1
                ins.then_inc(dchain, 1)
                dve.wait_ge(dchain, chain[0])

            v.memset(small[:, 0:45], 0.0)
            dve.wait_ge(dst_in, 16)
            dst_t = raw[:, 1, :].rearrange("p (g e) -> p g e", g=EG)
            link(v.tensor_reduce(dmax, dst_t, AX.X, ALU.max))
            dve.wait_ge(iotas, 1)
            blk3 = iota_blk[0:EP, :].unsqueeze(1).broadcast_to([EP, EG, NB])
            v.tensor_tensor(ind[:, :, :], blk3, dmax.unsqueeze(2).broadcast_to([EP, EG, NB]), ALU.is_gt).then_inc(find, 1)
            v.tensor_reduce(dmin, dst_t, AX.X, ALU.min)
            dve.wait_ge(fcnt, 1)
            link(v.tensor_scalar(fcol[:, :], psX[:, 0:NB], float(ET - SL), None, ALU.min))
            v.tensor_copy(f_i32[:, 0:NB], fcol[:, :]).then_inc(first_in, 1)
            for c in range(NT):
                m = ROWS[c]
                dve.wait_ge(x_in[c], 16)
                link(v.bn_stats(stats[0:m, c, :], h32[0:m, c, :]))
                v.bn_aggr(mv[0:m, c, :], stats[0:m, c, :]).then_inc(xstat, 1)
            dve.wait_ge(edges_in, 16 * 3)
            v.scalar_tensor_tensor(out=TF[:, 1, :], in0=raw[:, 1, :], scalar=float(R), in1=raw[:, 2, :],
                                   op0=ALU.mult, op1=ALU.add)
            dve.wait_ge(w_high_in, 2)
            link(v.tensor_tensor(TF[:, 3, :], raw[:, 3, :].bitcast(F32), TF[:, 2, :], ALU.subtract))
            v.tensor_scalar(TF[:, 3, :], TF[:, 3, :], LO_SCALE, None, ALU.mult).then_inc(efields, 1)
            dve.wait_ge(xrstd, 1)
            v.scalar_tensor_tensor(out=nmr, in0=mv[:, :, 0], scalar=-1.0, in1=rstd, op0=ALU.mult,
                                   op1=ALU.mult).then_inc(xnmr, 1)
            dve.wait_ge(eT, 1)
            for b in range(2):
                i = v.tensor_copy(
                    fields[0:EK, 2 * b:2 * b + 2, :].rearrange("e f (p g) -> e f g p", g=EG),
                    psG[0:EK, b, 0:2 * ET].rearrange("e (f g p) -> e f g p", f=2, g=EG))
                i.then_inc(turned, 1)

            def count_misses():
                link(v.tensor_scalar(dminm, dmin, float(-BW), None, ALU.add))
                link(v.tensor_tensor(ov[:, :, :], blk3, dminm.unsqueeze(2).broadcast_to([EP, EG, NB]), ALU.is_gt))
                v.tensor_tensor(ov[:, :, :], ov[:, :, :], ind[:, :, :], ALU.is_gt)
                link(v.tensor_tensor(uu[:, :, :], fcol[0:EP, :].unsqueeze(1).broadcast_to([EP, EG, NB]),
                                     negt.unsqueeze(2).broadcast_to([EP, EG, NB]), ALU.add))
                link(v.scalar_tensor_tensor(out=u2[:, :, :], in0=uu[:, :, :], scalar=float(SL - 1), in1=uu[:, :, :],
                                            op0=ALU.add, op1=ALU.mult))
                link(v.scalar_tensor_tensor(out=vv[:, :, :], in0=u2[:, :, :], scalar=1.0, in1=ov[:, :, :],
                                            op0=ALU.is_gt, op1=ALU.mult))
                v.tensor_reduce(vsum, vv[:, :, :], AX.XY, ALU.add).then_inc(viol, 1)

            def pick(b, first):
                v.tensor_tensor(slot[0:EK, b % 2, :, :], fields[0:EK, :, bass.ds(first, SL)],
                                key_off[0:EK, b, :].unsqueeze(2).broadcast_to([EK, 4, SL]), ALU.subtract).then_inc(gath, 1)

            def build(b):
                dve.wait_ge(gath, b + 1)
                f = slot[0:EK, b % 2, :, :]
                v.tensor_tensor(keq[0:EK, :, :], iota_key[0:EK, :].unsqueeze(1).broadcast_to([EK, SL, BC]),
                                f[:, 1, :].unsqueeze(2).broadcast_to([EK, SL, BC]), ALU.is_equal).then_inc(keq_in, 1)
                if b >= 2:
                    dve.wait_ge(blk_used, b - 1)
                s0 = (b % 2) * SL
                for j in range(SL):
                    v.tensor_scalar(onehot[0:EK, s0 + j, :], iota_src[0:EK, :], f[:, 0, j:j + 1], None, ALU.is_equal)
                dve.wait_ge(keq_in, b + 1)
                v.tensor_tensor(wkey[0:EK, s0:s0 + SL, :].rearrange("e s (h n) -> e s h n", h=2),
                                keq[0:EK, :, :].unsqueeze(2).broadcast_to([EK, SL, 2, BC]),
                                f[:, 2:4, :].rearrange("e h s -> e s h").unsqueeze(3).broadcast_to([EK, SL, 2, BC]),
                                ALU.mult).then_inc(blk_in, 1)

            def low_A(q):
                dve.wait_ge(AT_a, q + 1)
                if q >= 2:
                    dve.wait_ge(G_ps, q - 1)
                v.tensor_tensor(AT_lo[:, q % 2, :, :], A32[:, :, :], f32(AT_hi[:, q % 2, :, :]),
                                ALU.subtract).then_inc(AT_b, 1)

            def firsts(q):
                return [dve.value_load(f_i32[0:1, HB * q + i:HB * q + i + 1], min_val=0, max_val=ET - SL)
                        for i in range(HB)]

            def evac_A(q):
                dve.wait_ge(A_lo_ev, q + 1)
                v.tensor_tensor(A32[:, :, :], psA[:, :, 0:HC], A32[:, :, :], ALU.add).then_inc(A_ev, 1)

            def evac_G(q):
                h = q % 2
                dve.wait_ge(G_a, q + 1)
                v.tensor_tensor(G_lo[:, :, :, h * HD:(h + 1) * HD], psGk.rearrange("p k (d r) -> p k r d", r=R),
                                f32(G_hi[:, :, :, h * HD:(h + 1) * HD]), ALU.subtract).then_inc(G_b, 1)

            def evac_D(q):
                h = q % 2
                dve.wait_ge(D_ps, q + 1)
                if q % 2 == 0 and q >= 2:
                    dve.wait_ge(W_ps, q // 2)
                v.tensor_tensor(dm[:, :], psX[0:R, 0:HC], mask_r[:, :], ALU.mult).then_inc(D_m, 1)
                dve.wait_ge(D_m, q + 1)
                v.tensor_reduce(D4[:, h * HD:(h + 1) * HD], dm[:, :].rearrange("k (d r) -> k d r", r=R),
                                AX.X, ALU.add).then_inc(D_ev, 1)

            def inv_deg(c):
                m = ROWS[c]
                dve.wait_ge(deg_ps, c + 1)
                v.tensor_scalar(rdeg[0:m, c:c + 1], psG[0:m, 0, 0:1], 1.0, None, ALU.max).then_inc(deg_m, 1)
                dve.wait_ge(deg_m, c + 1)
                v.reciprocal(rdeg[0:m, c:c + 1], rdeg[0:m, c:c + 1]).then_inc(deg_ev, 1)

            def ln1_a(c):
                m = ROWS[c]
                dve.wait_ge(W_ps, c + 1)
                dve.wait_ge(deg_ev, c + 1)
                if c >= 1:
                    dve.wait_ge(x1_in, c)
                v.scalar_tensor_tensor(out=tbuf[0:m, :], in0=psX[0:m, :], scalar=rdeg[0:m, c:c + 1],
                                       in1=x1[0:m, c, :], op0=ALU.mult, op1=ALU.add).then_inc(t_out, 1)
                dve.wait_ge(t_out, 2 * c + 1)
                v.bn_stats(st1[0:m], tbuf[0:m, :]).then_inc(t_out, 1)
                dve.wait_ge(t_out, 2 * c + 2)
                v.bn_aggr(mv1[0:m], st1[0:m]).then_inc(ln1_v, 1)

            def ln1_b_(c):
                m = ROWS[c]
                dve.wait_ge(ln1_r, c + 1)
                v.scalar_tensor_tensor(out=nm1[0:m], in0=mv1[0:m, 0:1], scalar=-1.0, in1=rs1[0:m],
                                       op0=ALU.mult, op1=ALU.mult).then_inc(ln1_n, 1)

            def turn_low(c):
                m = ROWS[c]
                dve.wait_ge(xT_a, c + 1)
                v.tensor_tensor(x1T_lo[:, :, c * P:c * P + m],
                                psX[:, :].rearrange("p (k m) -> p k m", k=KD)[:, :, 0:m],
                                f32(x1T_hi[:, :, c * P:c * P + m]), ALU.subtract).then_inc(xT_b, 1)

            def general(q):
                with dve.If(flag > 0):
                    dve.wait_ge(blk_used, HB * (q + 1))
                    with dve.Fori(0, ET) as t:
                        v.tensor_copy(gslot[0:EK, :], fields[0:EK, :, bass.ds(t, 1)].squeeze(2)).then_inc(gen_m, 1)
                        dve.wait_ge(gen_m, t * 2 + (q * ET * 2 + 1))
                        v.tensor_scalar(gslot[0:EK, 1:2], gslot[0:EK, 1:2], float(q * HC), None,
                                        ALU.subtract).then_inc(gen_m, 1)
                        dve.wait_ge(gen_m, t * 2 + (q * ET * 2 + 2))
                        v.tensor_scalar(onehot[0:EK, 0, :], iota_src[0:EK, :], gslot[0:EK, 0:1], None, ALU.is_equal)
                        for part in range(2):
                            i = v.tensor_scalar(gkey[0:EK, part * HC:(part + 1) * HC], iota_src[0:EK, 0:HC],
                                                gslot[0:EK, 1:2], gslot[0:EK, 2 + part:3 + part],
                                                ALU.is_equal, ALU.mult)
                        i.then_inc(gen_in, 1)
                        dve.wait_ge(gen_used, t + (q * ET + 1))

            dve.wait_ge(first_in, 1)
            r = firsts(0)

            def self_low(c):
                m = ROWS[c]
                dve.wait_ge(hT_a, c + 1)
                v.tensor_tensor(hT[c % 2][:, 1, :, 0:m], psG[:, 0, :].rearrange("p (k m) -> p k m", k=KD)[:, :, 0:m],
                                f32(hT[c % 2][:, 0, :, 0:m]), ALU.subtract).then_inc(hT_b, 1)

            def self_add(c):
                m = ROWS[c]
                dve.wait_ge(self_ps, c + 1)
                dve.wait_ge(h_bs, c + 1)
                v.tensor_tensor(x1[0:m, c, :], self_bank(c)[0:m], x1[0:m, c, :], ALU.add).then_inc(self_ev, 1)

            def next_block(b):
                pick(b, r[b % HB])
                build(b)

            dve.wait_ge(turned, 2)
            next_block(0)
            next_block(1)
            count_misses()
            dve.wait_ge(vcnt, 1)
            v.tensor_copy(f_i32[:, NB:NB + 1], psX[:, 64:65]).then_inc(regs_in, 1)
            self_low(0)
            self_low(1)
            next_block(2)
            self_add(0)
            self_low(2)
            self_add(1)
            self_low(3)
            next_block(3)
            dve.wait_ge(regs_in, 1)
            flag = dve.value_load(f_i32[0:1, NB:NB + 1], min_val=0, max_val=1 << 20)
            self_add(2)
            self_low(4)
            self_add(3)
            self_add(4)
            v.memset(f32(x1T_hi[:, :, N:NP]), 0.0)
            v.memset(f32(x1T_lo[:, :, N:NP]), 0.0).then_inc(xpad, 1)
            general(0)
            r = firsts(1)
            next_block(HB)
            evac_A(0)
            next_block(HB + 1)
            low_A(0)
            next_block(HB + 2)
            next_block(HB + 3)
            general(1)
            for q in range(NQ):
                c, b = q // 2, HB * (q + 2)
                after, more = q + 1 < NQ, q + 2 < NQ
                if more:
                    r = firsts(q + 2)
                if q % 2 == 0:
                    if q >= 2:
                        turn_low(c - 1)
                else:
                    evac_G(q)
                    evac_D(q)
                    inv_deg(c)
                if more:
                    next_block(b)
                if after:
                    evac_A(q + 1)
                if more:
                    next_block(b + 1)
                if q % 2 == 0:
                    evac_G(q)
                    evac_D(q)
                if after:
                    low_A(q + 1)
                if q % 2 == 1 and after:
                    ln1_a(c)
                if more:
                    next_block(b + 2)
                if q % 2 == 1 and after:
                    ln1_b_(c)
                if more:
                    next_block(b + 3)
                    general(q + 2)
            for u in range(U_REL, U_W1):
                low_part(dve, u)
            ln1_a(NT - 1)
            ln1_b_(NT - 1)
            turn_low(NT - 1)
            i = 0
            for g0, n in FG:
                for f in range(KF):
                    dve.wait_ge(U_g, i + 1)
                    v.tensor_copy(u_hi[:, f, g0:g0 + n], u32[:, i % 2, 0:n]).then_inc(U_a, 1)
                    dve.wait_ge(U_a, i + 1)
                    v.tensor_tensor(u_lo[:, f, g0:g0 + n], u32[:, i % 2, 0:n], f32(u_hi[:, f, g0:g0 + n]),
                                    ALU.subtract).then_inc(U_b, 1)
                    i += 1
            for c in range(NT):
                m, b = ROWS[c], c % 2
                dve.wait_ge(Y_ps, c + 1)
                dve.wait_ge(x1b, c + 1)
                link(v.tensor_tensor(t2buf[0:m, b, :], ybank(c)[0:m], x1[0:m, c, :], ALU.add))
                link(v.bn_stats(st2[0:m, b, :], t2buf[0:m, b, :]))
                v.bn_aggr(mv2[0:m, b, :], st2[0:m, b, :]).then_inc(ln2_v, 1)
                dve.wait_ge(ln2_r, c + 1)
                v.scalar_tensor_tensor(out=nm2[0:m, b:b + 1], in0=mv2[0:m, b, 0:1], scalar=-1.0, in1=rs2[0:m, b:b + 1],
                                       op0=ALU.mult, op1=ALU.mult).then_inc(ln2_n, 1)
                dve.wait_ge(y_hat, c + 1)
                v.tensor_tensor(t2buf[0:m, b, :], t2buf[0:m, b, :], g2_bc[0:m, :], ALU.mult).then_inc(y_g, 1)
                dve.wait_ge(y_g, c + 1)
                if c >= 2:
                    dve.wait_ge(out_done[b], 16 * (c // 2))
                v.tensor_tensor(ybuf[0:m, b, :], t2buf[0:m, b, :], x_again[0:m, c, :], ALU.add).then_inc(y_out, 1)

        @block.tensor
        def _(pe):
            def mm(o, l, r, start, stop=False):
                return nc.tensor.matmul(o, l, r, start=start, stop=stop, skip_group_check=True)

            pe.wait_ge(iotas, 1)
            pe.wait_ge(find, 1)
            for g in range(EG):
                i = mm(psX[:, 0:NB], ones[0:EP, :], ind[:, g, :], g == 0, g == EG - 1)
            i.then_inc(fcnt, 1)
            pe.wait_ge(efields, 1)
            pe.wait_ge(srcs, 1)
            for f in range(4):
                for g in range(EG):
                    c0 = (f % 2) * ET + g * EP
                    i = nc.tensor.transpose(psG[0:EK, f // 2, c0:c0 + EP], TF[:, f, g * EK:(g + 1) * EK],
                                            ident[0:EP, 0:EP])
            i.then_inc(eT, 1)


            def turn_h(c):
                m = ROWS[c]
                pe.wait_ge(h_act, 2 * (c + 1))
                if c >= 1:
                    pe.wait_ge(hT_b, c)
                for k in range(KD):
                    i = nc.tensor.transpose(psG[:, 0, k * P:k * P + m], h32[0:m, c, k * P:(k + 1) * P],
                                            ident[0:m, 0:m])
                i.then_inc(hT_ps, 1)

            def self_product(c):
                m = ROWS[c]
                pe.wait_ge(hT_b, c + 1)
                pe.wait_ge(w_lo, U_SELF)
                if c >= 2:
                    pe.wait_ge(self_ev, c - 1)
                t, o = hT[c % 2], self_bank(c)[0:m]
                for k in range(KD):
                    mm(o, t[:, 0, k, 0:m], wself_hi[:, k, :], k == 0)
                    mm(o, t[:, 1, k, 0:m], wself_hi[:, k, :], False)
                    i = mm(o, t[:, 0, k, 0:m], wself_lo[:, k, :], False, k == KD - 1)
                i.then_inc(self_ps, 1)

            def build(q, blocks):
                for i in blocks:
                    b = HB * q + i
                    pe.wait_ge(blk_in, b + 1)
                    for j in range(SL):
                        s = (b % 2) * SL + j
                        for t in range(NT):
                            o = psA[:, t, :].rearrange("p (h n) -> p h n", h=2)[:, :, i * BC:(i + 1) * BC]
                            last = mm(o, onehot[0:EK, s, t * P:(t + 1) * P], wkey[0:EK, s, :],
                                      i == 0 and j == 0, i == HB - 1 and j == SL - 1)
                    last.then_inc(blk_used, 1)

            def finish_A(q):
                with pe.If(flag > 0):
                    pe.wait_ge(gen_in, q * ET + 1)
                    general_tile(True).then_inc(gen_used, 1)
                    with pe.Fori(1, ET) as t:
                        pe.wait_ge(gen_in, t + (q * ET + 1))
                        general_tile(False).then_inc(gen_used, 1)
                mm(psA[0:64, NT - 1, 0:2], zeros[:, :], zeros[:, 0:2], False, True).then_inc(A_ps, 1)

            def general_tile(start):
                for t in range(NT):
                    i = mm(psA[:, t, :], onehot[0:EK, 0, t * P:(t + 1) * P], gkey[0:EK], start)
                return i

            def G_hi_A(q):
                pe.wait_ge(AT_a, q + 1)
                for k in range(KD):
                    for s in range(NT):
                        m = ROWS[s]
                        mm(psGk[:, k, :], h_hi[0:m, s, k * P:(k + 1) * P], AT_hi[0:m, q % 2, s, :], k % 2 == 0 and s == 0)
                        mm(psGk[:, k, :], h_lo[0:m, s, k * P:(k + 1) * P], AT_hi[0:m, q % 2, s, :], False)

            def G_lo_A(q):
                pe.wait_ge(AT_b, q + 1)
                for k in range(KD):
                    for s in range(NT):
                        m = ROWS[s]
                        last = mm(psGk[:, k, :], h_hi[0:m, s, k * P:(k + 1) * P], AT_lo[0:m, q % 2, s, :], False,
                                  s == NT - 1)
                last.then_inc(G_ps, 1)

            def degrees(q):
                pe.wait_ge(A_s, q + 1)
                if q >= 1:
                    pe.wait_ge(D_ev, q)
                mm(psX[:, 0:HC], ones[:, :], A_sum[:, :], True, True).then_inc(D_ps, 1)

            def turn_x1(c):
                m = ROWS[c]
                pe.wait_ge(x1_in, c + 1)
                for k in range(KD):
                    i = nc.tensor.transpose(psX[:, k * P:k * P + m], x1[0:m, c, k * P:(k + 1) * P], ident[0:m, 0:m])
                i.then_inc(xT_ps, 1)

            def rel_product(c):
                m = ROWS[c]
                pe.wait_ge(D_ev, 2 * c + 2)
                pe.wait_ge(G_b, 2 * c + 2)
                mm(psG[0:m, 0, 0:1], D4[:, 0:m], ones[0:R, 0:1], True, True).then_inc(deg_ps, 1)
                mm(psX[0:m, :], D4[:, 0:m], brel_sb[:, :], True)
                for r in range(R):
                    if c == 0:
                        pe.wait_ge(w_lo, U_SELF + 2 * (r + 1))
                    for k in range(KD):
                        mm(psX[0:m, :], G_hi[:, k, r, 0:m], wrel_hi[:, r, k, :], False)
                        mm(psX[0:m, :], G_lo[:, k, r, 0:m], wrel_hi[:, r, k, :], False)
                        i = mm(psX[0:m, :], G_hi[:, k, r, 0:m], wrel_lo[:, r, k, :], False,
                               r == R - 1 and k == KD - 1)
                i.then_inc(W_ps, 1)

            build(0, range(2))
            pe.wait_ge(viol, 1)
            mm(psX[:, 64:65], ones[0:EP, :], vsum, True, True).then_inc(vcnt, 1)
            pe.wait_ge(turned, 2)
            pe.wait_ge(regs_in, 1)
            flag = pe.value_load(f_i32[0:1, NB:NB + 1], min_val=0, max_val=1 << 20)
            for c in range(NT):
                turn_h(c)
                if c >= 1:
                    self_product(c - 1)
            self_product(NT - 1)
            build(0, range(2, 4))
            finish_A(0)
            pe.wait_ge(self_ev, NT)
            pe.wait_ge(h_los, NT)
            for q in range(NQ):
                if q + 1 < NQ:
                    pe.wait_ge(A_ev, q + 1)
                    build(q + 1, range(0, 2))
                if q >= 1:
                    pe.wait_ge(G_b, q)
                if q >= 2 and q % 2 == 0:
                    pe.wait_ge(deg_ev, q // 2)
                G_hi_A(q)
                if q % 2 == 0:
                    if q >= 2:
                        turn_x1(q // 2 - 1)
                    build(q + 1, range(2, 4))
                    finish_A(q + 1)
                    G_lo_A(q)
                    if q >= 2:
                        pe.wait_ge(xT_b, q // 2)
                    degrees(q)
                else:
                    G_lo_A(q)
                    degrees(q)
                    if q + 1 < NQ:
                        build(q + 1, range(2, 4))
                        finish_A(q + 1)
                    rel_product(q // 2)
            i = 0
            for g, (g0, n) in enumerate(FG):
                if g == 1:
                    pe.wait_ge(xT_b, NT)
                    pe.wait_ge(xpad, 1)
                for f in range(KF):
                    if i == 0:
                        pe.wait_ge(w1_lo, KD)
                    if i == NT:
                        turn_x1(NT - 1)
                    if i >= NT:
                        pe.wait_ge(U_g, i - NT + 1)
                    o = psA[:, i % NT, 0:n]
                    for k in range(KD):
                        wh, wl = W1_hi[:, k, f * P:(f + 1) * P], W1_lo[:, k, f * P:(f + 1) * P]
                        mm(o, wh, x1T_hi[:, k, g0:g0 + n], k == 0)
                        mm(o, wh, x1T_lo[:, k, g0:g0 + n], False)
                        last = mm(o, wl, x1T_hi[:, k, g0:g0 + n], False, k == KD - 1)
                    last.then_inc(U_ps, 1)
                    i += 1
            pe.wait_ge(*split(NU - 1))
            for c in range(NT):
                m = ROWS[c]
                pe.wait_ge(U_b, KF if c < 3 else 2 * KF)
                if c >= 3:
                    pe.wait_ge(ln2_v, c - 2)
                o = ybank(c)[0:m]
                for f in range(KF):
                    uh, ul = u_hi[:, f, c * P:c * P + m], u_lo[:, f, c * P:c * P + m]
                    mm(o, uh, W2_hi[:, f, :], f == 0)
                    mm(o, ul, W2_hi[:, f, :], False)
                    last = mm(o, uh, W2_lo[:, f, :], False, f == KF - 1)
                last.then_inc(Y_ps, 1)


_INS = ["x", "src", "dst", "edge_type_4", "edge_weight", "L0_gnn_W_self", "L0_gnn_b_self", "L0_gnn_W_rel",
        "L0_gnn_b_rel", "L0_gnn_ln1_g", "L0_gnn_ln1_b", "L0_gnn_ln2_g", "L0_gnn_ln2_b", "L0_gnn_W_ffn1",
        "L0_gnn_b_ffn1", "L0_gnn_W_ffn2", "L0_gnn_b_ffn2"]


def kernel(**inputs):
    import numpy as np
    import concourse.bacc as bacc
    from concourse.bass_utils import run_bass_kernel_spmd as run

    nc = bacc.Bacc("TRN2", target_bir_lowering=False, num_devices=1)
    arrays, args = {}, []
    for name in _INS:
        a = np.ascontiguousarray(inputs[name])
        arrays[f"in_{name}"] = a
        args.append(nc.dram_tensor(f"in_{name}", a.shape, mybir.dt.from_np(a.dtype), kind="ExternalInput").ap())
    shape = inputs["x"].shape
    args.append(nc.dram_tensor("out_0", shape, F32, kind="ExternalOutput").ap())
    gnn_layer(nc, *args)
    r = run(nc, [arrays], core_ids=[0])
    return r.results[0]["out_0"]
```

```python
from contextlib import ExitStack

import concourse.bass as bass
from concourse import mybir


F32 = mybir.dt.float32
F32R = mybir.dt.float32r
F16 = mybir.dt.float16
I32 = mybir.dt.int32
ALU = mybir.AluOpType
ACT = mybir.ActivationFunctionType
AX = mybir.AxisListType

P = 128
LO_SCALE = 4096.0
EPS = 1e-5


def gnn_layer(nc, x, src, dst, etype, ew, W_self, b_self, W_rel, b_rel, ln1_g, ln1_b, ln2_g, ln2_b,
              W1, b1, W2, b2, out):
    N, D = x.shape
    E = src.shape[0]
    R = W_rel.shape[0]
    F = W1.shape[1]
    KD = D // P
    KF = F // P
    NT = -(-N // P)
    NP = NT * P
    ROWS = [min(P, N - c * P) for c in range(NT)]
    EK = N // 5
    ET = E // EK
    EG = 3
    EP = ET // EG
    BW = 16
    BC = BW * R
    NB = NP // BW
    HB = 4
    HC = HB * BC
    HD = HB * BW
    NQ = NB // HB
    SL = 6
    RATE = round(EK * N / E)
    LAG, LEAD = 7, 6
    WINDOW = [(max(0, RATE * j - LAG), min(BW, RATE * j + LEAD)) for j in range(SL)]
    WD = max(hi - lo for lo, hi in WINDOW)
    W0 = [min(lo, BW - WD) for lo, _ in WINDOW]
    WK = WD * R
    RING = 2 * SL
    LATE = 2 * HB
    assert EK * ET == E and EG * EP == ET and R * EK <= 512
    UC = 1024
    EARLY = 3
    FG = [(0, 3 * P), (3 * P, NP - 3 * P)]

    base = nc.sbuf_base + (-nc.sbuf_base) % 64

    def sb(name, shape, dt, kb):
        return nc.alloc_sbuf_tensor_at(name, shape, dt, offset=base + int(kb * 1024))

    wrel_hi = sb("wrel_hi", [P, R, KD, D], F32R, 0)
    wrel_lo = sb("wrel_lo", [P, R, KD, D], F32R, 32)
    wself_hi = sb("wself_hi", [P, KD, D], F32R, 64)
    wself_lo = sb("wself_lo", [P, KD, D], F32R, 72)
    x1T_hi = sb("x1T_hi", [P, KD, NP], F32R, 64)
    x1T_lo = sb("x1T_lo", [P, KD, NP], F32R, 74)
    onehot = sb("onehot", [P, RING, NP], F16, 84)
    wkey = sb("wkey", [P, RING, 2 * WK], F16, 99)
    gkey = sb("gkey", [P, 2 * HC], F16, 99)
    keq = sb("keq", [P, 2, SL, WK], F16, 202.25)
    iota_win = sb("iota_win", [P, SL, WK], F16, 203.5)
    AT_hi = sb("AT_hi", [P, 2, NT, HC], F32R, 102)
    AT_lo = sb("AT_lo", [P, 2, NT, HC], F32R, 112)
    A32 = sb("A32", [P, NT, HC], F32, 122)
    G_hi = sb("G_hi", [P, KD, R, P], F32R, 127)
    G_lo = sb("G_lo", [P, KD, R, P], F32R, 135)
    h32 = sb("h32", [P, NT, D], F32, 127)
    hT = [sb("hT0", [P, 2, KD, P], F32R, 56), sb("hT1", [P, 2, KD, P], F32R, 137)]
    h_hi = sb("h_hi", [P, NT, D], F32R, 143)
    h_lo = sb("h_lo", [P, NT, D], F32R, 153)
    x1 = sb("x1", [P, NT, D], F32, 163)
    bself_bc = sb("bself_bc", [P, D], F32, 173)
    g1_bc = sb("g1_bc", [P, D], F32, 175)
    b1_bc = sb("b1_bc", [P, D], F32, 177)
    stage = sb("stage", [P, 3, UC], F32, 179)
    onehot_3 = sb("onehot_3", [P, SL, NP], F16, 179)
    wkey_3 = sb("wkey_3", [P, SL, 2 * WK], F16, 186.5)
    fields = sb("fields", [P, 4, ET + SL], F32, 191)
    iota_src = sb("iota_src", [P, NP], F16, 193.75)
    zeros = sb("zeros", [P, 64], F16, 195.125)
    ident = sb("ident", [P, P], F32, 195.25)
    ones = sb("ones", [P, P], F32, 195.75)
    key_off = sb("key_off", [P, NB, 4], F32, 196.25)
    SB = 3
    slot = sb("slot", [P, SB, 4, SL], F32, 196.875)
    select = sb("select", [P, R, R], F32, 195)
    A_sum = sb("A_sum", [P, HC], F32, 197.25)
    brel_sb = sb("brel_sb", [R, D], F32, 198.25)
    tbuf = sb("tbuf", [P, D], F32, 200.25)
    D4 = sb("D4", [R, P], F32, 204.25)
    small = sb("small", [P, 160], F32, 204.75)
    away = sb("away", [P, NP], F16, 205.5)
    f_i32 = sb("f_i32", [P, NB + 8], I32, 206.75)
    raw = sb("raw", [EP, 4, EG * EK], I32, 102)
    TF = sb("TF", [EP, 4, EG * EK], F32, 108)
    w16 = sb("w16", [EP, EG * EK], F16, 114)
    iota_blk = sb("iota_blk", [P, NB], F32, 115)
    ind = sb("ind", [EP, EG, NB], F32, 115.25)
    ov = sb("ov", [EP, EG, NB], F32, 116)
    uu = sb("uu", [EP, EG, NB], F32, 116.5)
    from_min = sb("from_min", [EP, EG, NB], F32, 117)
    from_max = sb("from_max", [EP, EG, NB], F32, 117.5)
    miss = sb("miss", [EP, 3, EG, NB], F32, 118.25)
    fcol = sb("fcol", [P, NB], F32, 118)
    W1_hi = sb("W1_hi", [P, KD, F], F32R, 84)
    W1_lo = sb("W1_lo", [P, KD, F], F32R, 102)
    W2_hi = sb("W2_hi", [P, KF, D], F32R, 143)
    W2_lo = sb("W2_lo", [P, KF, D], F32R, 127)
    u_hi = sb("u_hi", [P, KF, NP], F32R, 0)
    u_lo = sb("u_lo", [P, KF, NP], F32R, 20)
    u32 = sb("u32", [P, 2, 3 * P], F32, 40)
    x_again = sb("x_again", [P, NT, D], F32, 44)
    g2_bc = sb("g2_bc", [P, D], F32, 54)
    b2_bc = sb("b2_bc", [P, D], F32, 56)
    bf2_bc = sb("bf2_bc", [P, D], F32, 58)
    ybuf = sb("ybuf", [P, 2, D], F32, 60)
    t2buf = sb("t2buf", [P, 2, D], F32, 122)

    stats = small[:, 0:30].rearrange("p (c s) -> p c s", s=6)
    mv = small[:, 30:40].rearrange("p (c s) -> p c s", s=2)
    rstd = small[:, 40:45]
    nmr = small[:, 45:50]
    mhalf = small[:, 50:55]
    var_e = small[:, 55:60]
    rdeg = small[:, 60:65]
    dmin = small[0:EP, 65:65 + EG]
    dmax = small[0:EP, 68:68 + EG]
    negt = small[0:EP, 132:132 + EG]
    vsum = small[0:EP, 135:136]
    bf1 = small[:, 76:76 + KF]
    st1 = small[:, 84:90]
    mv1 = small[:, 90:92]
    ve1 = small[:, 92:93]
    rs1 = small[:, 93:94]
    nm1 = small[:, 94:95]
    st2 = small[:, 100:112].rearrange("p (c s) -> p c s", s=6)
    mv2 = small[:, 112:116].rearrange("p (c s) -> p c s", s=2)
    ve2 = small[:, 116:118]
    rs2 = small[:, 118:120]
    gslot = small[:, 124:128]

    psA = nc.alloc_psum_tensor("psA", [P, NT, 512], F32)
    psG = nc.alloc_psum_tensor("psG", [P, 2, 512], F32)
    psX = nc.alloc_psum_tensor("psX", [P, 512], F32)

    ctx = ExitStack()
    with ctx:
        def sem(name):
            return ctx.enter_context(nc.semaphore(name))

        dst_in = sem("dst_in")
        edges_in = sem("edges_in")
        x_in = [sem(f"x_in{c}") for c in range(NT)]
        consts_in = sem("consts_in")
        stage_in = [sem(f"stage_in{i}") for i in range(3)]
        late_in = sem("late_in")
        out_done = [sem(f"out_done{i}") for i in range(2)]
        iotas = sem("iotas")
        blk_iotas = sem("blk_iotas")
        table_in = sem("table_in")
        dchain = sem("dchain")
        pchain = sem("pchain")
        w_high_in = sem("w_high_in")
        efields = sem("efields")
        srcs = sem("srcs")
        first_in = sem("first_in")
        eT = sem("eT")
        find = sem("find")
        fcnt = sem("fcnt")
        viol = sem("viol")
        vcnt = sem("vcnt")
        regs_in = sem("regs_in")
        xstat = sem("xstat")
        xrstd = sem("xrstd")
        xnmr = sem("xnmr")
        h_act = sem("h_act")
        h_his = sem("h_his")
        h_los = sem("h_los")
        h_bs = sem("h_bs")
        w_hi = sem("w_hi")
        w_lo = sem("w_lo")
        w_lo_dve = sem("w_lo_dve")
        hT_ps = sem("hT_ps")
        hT_a = sem("hT_a")
        hT_b = sem("hT_b")
        self_ps = sem("self_ps")
        turned = sem("turned")
        xpad = sem("xpad")
        self_ev = sem("self_ev")
        gath = sem("gath")
        oh_act = sem("oh_act")
        away_in = sem("away_in")
        keq_in = sem("keq_in")
        blk_in = sem("blk_in")
        blk_used = sem("blk_used")
        gen_in = sem("gen_in")
        gen_m = sem("gen_m")
        gen_used = sem("gen_used")
        A_ps = sem("A_ps")
        A_lo_ev = sem("A_lo_ev")
        A_ev = sem("A_ev")
        AT_a = sem("AT_a")
        AT_b = sem("AT_b")
        A_s = sem("A_s")
        G_ps = sem("G_ps")
        G_a = sem("G_a")
        G_b = sem("G_b")
        D_ps = sem("D_ps")
        D_ev = sem("D_ev")
        deg_ps = sem("deg_ps")
        deg_m = sem("deg_m")
        deg_ev = sem("deg_ev")
        W_ps = sem("W_ps")
        t_out = sem("t_out")
        ln1_s = sem("ln1_s")
        ln1_v = sem("ln1_v")
        ln1_r = sem("ln1_r")
        ln1_n = sem("ln1_n")
        xhat_in = sem("xhat_in")
        x1_in = sem("x1_in")
        xT_ps = sem("xT_ps")
        xT_a = sem("xT_a")
        xT_b = sem("xT_b")
        U_ps = sem("U_ps")
        U_g = sem("U_g")
        U_a = sem("U_a")
        U_b = sem("U_b")
        x1b = sem("x1b")
        Y_ps = sem("Y_ps")
        ln2_v = sem("ln2_v")
        ln2_r = sem("ln2_r")
        y_g = sem("y_g")
        y_out = sem("y_out")

        block = ctx.enter_context(nc.Block())

        units = []
        for k in range(0, KD, 2):
            units.append((W_self.rearrange("(k p) n -> p k n", p=P)[:, k:k + 2, :],
                          wself_hi[:, k:k + 2, :], wself_lo[:, k:k + 2, :]))
        for r in range(R):
            for k in range(0, KD, 2):
                units.append((W_rel[r].rearrange("(k p) n -> p k n", p=P)[:, k:k + 2, :],
                              wrel_hi[:, r, k:k + 2, :], wrel_lo[:, r, k:k + 2, :]))
        U_SELF, U_REL = 2, 2 + 2 * R
        for k in range(KD):
            units.append((W1[k * P:(k + 1) * P, :], W1_hi[:, k, :], W1_lo[:, k, :]))
        U_W1 = U_REL + KD
        for k in range(0, KF, 2):
            units.append((W2.rearrange("(k p) n -> p k n", p=P)[:, k:k + 2, :],
                          W2_hi[:, k:k + 2, :], W2_lo[:, k:k + 2, :]))
        NU = len(units)

        def stage_view(u):
            v = stage[:, u % 3, :]
            return v if U_REL <= u < U_W1 else v.rearrange("p (k n) -> p k n", k=2)

        def ring(b):
            i = b % 2 if b < LATE else (b - LATE) % 3
            if i == 2:
                return onehot_3[:, :, :], wkey_3[:, :, :]
            return onehot[:, i * SL:(i + 1) * SL, :], wkey[:, i * SL:(i + 1) * SL, :]

        def ring_free(eng, b):
            if b >= LATE + 3:
                eng.wait_ge(blk_used, b - 2)
            elif b == LATE + 2:
                eng.wait_ge(*split(U_REL - 1))
                eng.wait_ge(*split(U_REL - 2))
                eng.wait_ge(*split(1))
            elif b >= 2:
                eng.wait_ge(blk_used, b - 1)

        LAST_3 = max(b for b in range(LATE, NB) if (b - LATE) % 3 == 2)

        DVE_UNITS = [1] + list(range(U_REL, U_W1))
        POOL_UNITS = [u for u in range(NU) if u not in DVE_UNITS]

        def split(u):
            if u in DVE_UNITS:
                return w_lo_dve, DVE_UNITS.index(u) + 1
            return w_lo, POOL_UNITS.index(u) + 1

        def f32(ap):
            return ap.bitcast(F32)

        def G_banks(q):
            return (psG if q < NQ - 1 else psA[:, 0:2, :])[:, :, :].rearrange("p b (k n) -> p (b k) n", k=2)

        def U_bank(i):
            return psA[:, (i + 2) % NT, :]

        def self_bank(c):
            return [psX[:, :], psG[:, 1, :]][c % 2]

        def ybank(c):
            return [psG[:, 0, :], psG[:, 1, :], psX[:, :]][c % 3]

        def low_part(eng, u):
            eng.wait_ge(w_hi, u + 1)
            done = split(u)[0]
            eng.tensor_tensor(units[u][2], stage_view(u), f32(units[u][1]), ALU.subtract).then_inc(done, 1)

        def ln1_pool(c):
            g, pool, m = nc.gpsimd, nc.gpsimd, ROWS[c]
            pool.wait_ge(ln1_v, c + 1)
            g.tensor_scalar(ve1[0:m], mv1[0:m, 1:2], EPS, None, ALU.add).then_inc(ln1_s, 1)
            pool.wait_ge(ln1_s, 2 * c + 1)
            g.tensor_tensor(rs1[0:m], ve1[0:m], mhalf[0:m, 0:1], ALU.pow).then_inc(ln1_r, 1)
            pool.wait_ge(xhat_in, c + 1)
            g.tensor_tensor(tbuf[0:m, :], tbuf[0:m, :], g1_bc[0:m, :], ALU.mult).then_inc(ln1_s, 1)
            pool.wait_ge(ln1_s, 2 * c + 2)
            g.tensor_tensor(x1[0:m, c, :], tbuf[0:m, :], b1_bc[0:m, :], ALU.add).then_inc(x1_in, 1)

        def ln1_act(c):
            a, m = nc.scalar, ROWS[c]
            a.wait_ge(ln1_n, c + 1)
            a.activation(tbuf[0:m, :], tbuf[0:m, :], ACT.Identity, scale=rs1[0:m], bias=nm1[0:m]).then_inc(xhat_in, 1)

        def turn_act(c):
            a, m = nc.scalar, ROWS[c]
            a.wait_ge(xT_ps, c + 1)
            a.copy(x1T_hi[:, :, c * P:c * P + m],
                   psX[:, :].rearrange("p (k m) -> p k m", k=KD)[:, :, 0:m]).then_inc(xT_a, 1)

        @block.sync
        def _(sp):
            sp.dma_start(raw[:, 1, :], dst.rearrange("(p e) -> p e", p=EP)).then_inc(dst_in, 16)
            sp.dma_start(raw[:, 2, :], etype.rearrange("(p e) -> p e", p=EP)).then_inc(edges_in, 16)
            for c in range(NT):
                sp.dma_start(h32[0:ROWS[c], c, :], x[c * P:c * P + ROWS[c], :]).then_inc(x_in[c], 16)
            for u in range(NU):
                if u == 3:
                    for buf, vec in ((bself_bc, b_self), (g1_bc, ln1_g), (b1_bc, ln1_b)):
                        row = vec.rearrange("(a d) -> a d", a=1)
                        sp.dma_start(buf[:, :], row.broadcast_to([P, D])).then_inc(consts_in, 16)
                    sp.dma_start(brel_sb[:, :], b_rel).then_inc(consts_in, 16)
                    with nc.allow_non_contiguous_dma("bias by partition"):
                        sp.dma_start(bf1, b1.rearrange("(f p) -> p f", p=P)).then_inc(consts_in, 16)
                if u >= 3:
                    sp.wait_ge(*split(u - 3))
                if u == U_REL:
                    sp.wait_ge(blk_used, LAST_3 + 1)
                sp.dma_start(stage_view(u), units[u][0]).then_inc(stage_in[u % 3], 16)
            sp.wait_ge(W_ps, NT)
            for c in range(NT):
                sp.dma_start(x_again[0:ROWS[c], c, :], x[c * P:c * P + ROWS[c], :]).then_inc(late_in, 16)
            for buf, v in ((g2_bc, ln2_g), (b2_bc, ln2_b), (bf2_bc, b2)):
                sp.dma_start(buf[:, :], v.rearrange("(a d) -> a d", a=1).broadcast_to([P, D])).then_inc(late_in, 16)
            for c in range(NT):
                sp.wait_ge(y_out, c + 1)
                sp.dma_start(out[c * P:c * P + ROWS[c], :], ybuf[0:ROWS[c], c % 2, :]).then_inc(out_done[c % 2], 16)
            for i in range(2):
                sp.wait_ge(out_done[i], 16 * len(range(i, NT, 2)))

        @block.gpsimd
        def _(pool):
            chain = [0]

            def link(ins):
                chain[0] += 1
                ins.then_inc(pchain, 1)
                pool.wait_ge(pchain, chain[0])

            g = nc.gpsimd
            g.iota(iota_blk[:, :], [[BW, NB]], base=0, channel_multiplier=0, allow_small_or_imprecise_dtypes=True)
            g.iota(negt, [[-1, EG]], base=0, channel_multiplier=-EG, allow_small_or_imprecise_dtypes=True)
            g.memset(mhalf, -0.5)
            g.memset(ones[:, :], 1.0).then_inc(blk_iotas, 1)
            g.iota(iota_src[:, :], [[1, NP]], base=0, channel_multiplier=0, allow_small_or_imprecise_dtypes=True)
            for j in range(SL):
                g.iota(iota_win[:, j, :], [[1, WK]], base=W0[j] * R, channel_multiplier=0,
                       allow_small_or_imprecise_dtypes=True)
            link(g.memset(key_off[:, :, :], 0.0))
            g.iota(key_off[:, :, 1], [[BC, NB]], base=0, channel_multiplier=0, allow_small_or_imprecise_dtypes=True)
            link(g.memset(ident[:, :], 0.0))
            g.affine_select(out=ident[:, :], in_=ident[:, :], compare_op=ALU.not_equal, fill=1.0, base=0,
                            pattern=[[-1, P]], channel_multiplier=1)
            link(g.memset(select[:, :, :], 0.0))
            for r in range(R):
                g.memset(select[:, r, r:r + 1], 1.0)
            g.memset(zeros[:, :], 0.0).then_inc(iotas, 1)
            pool.wait_ge(xstat, 1)
            link(g.tensor_scalar(var_e, mv[:, :, 1], EPS, None, ALU.add))
            g.tensor_tensor(rstd, var_e, mhalf, ALU.pow).then_inc(xrstd, 1)
            low_part(pool, 0)
            pool.wait_ge(consts_in, 16 * 5)
            for c in range(NT):
                m = ROWS[c]
                pool.wait_ge(h_act, c + 1)
                g.tensor_tensor(x1[0:m, c, :], h32[0:m, c, :], bself_bc[0:m, :], ALU.add).then_inc(h_bs, 1)
            for c in range(NT):
                m = ROWS[c]
                pool.wait_ge(h_his, c + 1)
                g.tensor_tensor(h_lo[0:m, c, :], h32[0:m, c, :], f32(h_hi[0:m, c, :]), ALU.subtract).then_inc(h_los, 1)

            def sum_A(q):
                pool.wait_ge(A_ev, q + 1)
                if q >= 1:
                    pool.wait_ge(D_ps, q)
                link(g.tensor_tensor(A_sum[:, :], A32[:, 0, :], A32[:, 1, :], ALU.add))
                for s in range(2, NT):
                    i = g.tensor_tensor(A_sum[:, :], A_sum[:, :], A32[:, s, :], ALU.add)
                    if s < NT - 1:
                        link(i)
                i.then_inc(A_s, 1)

            for u in range(U_SELF, U_REL):
                if u == U_REL - 3:
                    sum_A(0)
                if u == U_REL - 2:
                    pool.wait_ge(self_ps, NT)
                low_part(pool, u)
            for q in range(1, NQ):
                sum_A(q)
                if q % 2 == 0:
                    ln1_pool(q // 2 - 1)
            ln1_pool(NT - 1)
            pool.wait_ge(W_ps, NT)
            for u in range(U_W1, NU):
                low_part(pool, u)
            pool.wait_ge(late_in, 16 * (NT + 3))
            for c in range(NT):
                m = ROWS[c]
                pool.wait_ge(xT_ps, c + 1)
                g.tensor_tensor(x_again[0:m, c, :], x_again[0:m, c, :], b2_bc[0:m, :], ALU.add)
                g.tensor_tensor(x1[0:m, c, :], x1[0:m, c, :], bf2_bc[0:m, :], ALU.add).then_inc(x1b, 1)
            for c in range(NT):
                m, b = ROWS[c], c % 2
                pool.wait_ge(ln2_v, c + 1)
                link(g.tensor_scalar(ve2[0:m, b:b + 1], mv2[0:m, b, 1:2], EPS, None, ALU.add))
                g.tensor_tensor(rs2[0:m, b:b + 1], ve2[0:m, b:b + 1], mhalf[0:m, 0:1], ALU.pow).then_inc(ln2_r, 1)

        @block.scalar
        def _(act):
            a = nc.scalar
            act.dma_start(raw[:, 3, :], ew.bitcast(I32).rearrange("(p e) -> p e", p=EP)).then_inc(edges_in, 16)
            act.dma_start(raw[:, 0, :], src.rearrange("(p e) -> p e", p=EP)).then_inc(edges_in, 16)

            def high_part(u):
                act.wait_ge(stage_in[u % 3], 16 * (u // 3 + 1))
                if u == U_REL:
                    act.wait_ge(blk_used, NB)
                if u == U_W1:
                    act.wait_ge(G_ps, 2 * NQ)
                a.copy(units[u][1], stage_view(u)).then_inc(w_hi, 1)

            act.wait_ge(blk_iotas, 1)
            a.activation(nm1, ones[:, 0:1], ACT.Relu).then_inc(table_in, 1)
            act.wait_ge(edges_in, 16 * 3)
            a.copy(w16[:, :], raw[:, 3, :].bitcast(F32)).then_inc(w_high_in, 1)
            act.wait_ge(w_high_in, 1)
            a.copy(TF[:, 2, :], w16[:, :]).then_inc(w_high_in, 1)
            a.copy(TF[:, 0, :], raw[:, 0, :]).then_inc(srcs, 1)
            high_part(0)
            high_part(1)
            act.wait_ge(xnmr, 1)

            def h_of(c):
                m = ROWS[c]
                a.activation(h32[0:m, c, :], h32[0:m, c, :], ACT.Relu, scale=rstd[0:m, c:c + 1],
                             bias=nmr[0:m, c:c + 1]).then_inc(h_act, 1)

            def h_high(c):
                a.copy(h_hi[0:ROWS[c], c, :], h32[0:ROWS[c], c, :]).then_inc(h_his, 1)

            def hT_high(c):
                m = ROWS[c]
                act.wait_ge(hT_ps, c + 1)
                if c >= 2:
                    act.wait_ge(self_ps, c - 1)
                a.copy(hT[c % 2][:, 0, :, 0:m],
                       psG[:, 0, :].rearrange("p (k m) -> p k m", k=KD)[:, :, 0:m]).then_inc(hT_a, 1)

            def onehot_last(b):
                act.wait_ge(gath, b + 1)
                if b == 0:
                    act.wait_ge(iotas, 1)
                ring_free(act, b)
                if b >= 1:
                    act.wait_ge(oh_act, b)
                a.activation(away[0:EK, :], iota_src[0:EK, :], ACT.Abs, scale=-1.0,
                             bias=slot[0:EK, b % SB, 0, SL - 1:SL]).then_inc(away_in, 1)
                act.wait_ge(away_in, b + 1)
                a.activation(ring(b)[0][0:EK, SL - 1, :], away[0:EK, :], ACT.Relu, scale=-1.0,
                             bias=ones[0:EK, 0:1]).then_inc(oh_act, 1)

            h_of(0)
            h_of(1)
            hT_high(0)
            for c in range(2, NT):
                h_of(c)
            hT_high(1)
            onehot_last(0)
            onehot_last(1)
            high_part(U_SELF)
            act.wait_ge(h_act, NT)
            for c in range(NT):
                h_high(c)
            for c in range(2, NT):
                hT_high(c)
                onehot_last(c)
                if c < HB:
                    high_part(U_SELF + c - 1)

            def A_low_weights(q):
                act.wait_ge(A_ps, q + 1)
                if q >= 1:
                    act.wait_ge(A_s, q)
                    act.wait_ge(AT_b, q)
                a.mul(A32[:, :, :], psA[:, :, HC:2 * HC], 1.0 / LO_SCALE).then_inc(A_lo_ev, 1)

            def A_high(q):
                act.wait_ge(A_ev, q + 1)
                if q >= 2:
                    act.wait_ge(G_ps, 2 * (q - 1))
                a.copy(AT_hi[:, q % 2, :, :], A32[:, :, :]).then_inc(AT_a, 1)

            def G_high(q, banks):
                act.wait_ge(G_ps, 2 * q + banks[-1] + 1)
                if q == 0:
                    act.wait_ge(h_bs, NT)
                    act.wait_ge(h_los, NT)
                    act.wait_ge(self_ps, NT)
                if q % 2 == 0 and q >= 2:
                    act.wait_ge(W_ps, q // 2)
                h, k0, k1 = q % 2, 2 * banks[0], 2 * banks[-1] + 2
                a.copy(G_hi[:, k0:k1, :, h * HD:(h + 1) * HD],
                       G_banks(q)[:, k0:k1, :].rearrange("p k (d r) -> p k r d", r=R)).then_inc(G_a, len(banks))

            A_low_weights(0)
            onehot_last(HB + 1)
            A_high(0)
            high_part(U_SELF + NT - 2)
            for u in range(U_SELF + NT - 1, U_REL):
                high_part(u)
                if u < U_SELF + NT + 1:
                    onehot_last(u - (U_SELF + NT - 1) + HB + 2)
            for q in range(NQ):
                b, after, more = HB * (q + 2), q + 1 < NQ, q + 2 < NQ
                if q % 2 == 0:
                    if more:
                        onehot_last(b)
                    G_high(q, [0])
                    A_low_weights(q + 1)
                    if q >= 2:
                        turn_act(q // 2 - 1)
                    A_high(q + 1)
                    G_high(q, [1])
                    if more:
                        onehot_last(b + 1)
                        onehot_last(b + 2)
                    else:
                        for u in range(U_REL, U_REL + KD - 1):
                            high_part(u)
                else:
                    G_high(q, [0, 1])
                    if more:
                        onehot_last(b)
                    if after:
                        A_low_weights(q + 1)
                        A_high(q + 1)
                    if more:
                        onehot_last(b + 1)
                        onehot_last(b + 2)
                if more:
                    onehot_last(b + 3)
                if q % 2 == 1 and after:
                    ln1_act(q // 2)
            for u in range(U_REL + KD - 1, NU - 1):
                high_part(u)
            ln1_act(NT - 1)
            i = 0
            for g0, n in FG:
                for f in range(KF):
                    if i == NT:
                        turn_act(NT - 1)
                    act.wait_ge(U_ps, i + 1)
                    if i >= 2:
                        act.wait_ge(U_b, i - 1)
                    a.activation(u32[:, i % 2, 0:n], U_bank(i)[:, 0:n], ACT.Gelu,
                                 bias=bf1[:, f:f + 1]).then_inc(U_g, 1)
                    if i == NT + 1:
                        high_part(NU - 1)
                    i += 1

        @block.vector
        def _(dve):
            v = nc.vector
            chain = [0]

            def link(ins):
                chain[0] += 1
                ins.then_inc(dchain, 1)
                dve.wait_ge(dchain, chain[0])

            def firsts(q):
                return [dve.value_load(f_i32[0:1, HB * q + i:HB * q + i + 1], min_val=0, max_val=ET)
                        for i in range(HB)]

            v.memset(small[:, 0:45], 0.0)
            dve.wait_ge(dst_in, 16)
            dst_t = raw[:, 1, :].rearrange("p (g e) -> p g e", g=EG)
            link(v.tensor_reduce(dmax, dst_t, AX.X, ALU.max))
            dve.wait_ge(blk_iotas, 1)
            blk3 = iota_blk[0:EP, :].unsqueeze(1).broadcast_to([EP, EG, NB])
            dmax3 = dmax.unsqueeze(2).broadcast_to([EP, EG, NB])
            v.tensor_tensor(ind[:, :, :], blk3, dmax3, ALU.is_gt).then_inc(find, 1)
            dve.wait_ge(fcnt, 1)
            v.tensor_copy(f_i32[:, 0:NB], psX[:, 0:NB]).then_inc(first_in, 1)
            v.tensor_copy(fcol[:, :], psX[:, 0:NB]).then_inc(first_in, 1)
            v.memset(fields[:, :, ET:ET + SL], -1.0)

            def row_stats(c):
                dve.wait_ge(x_in[c], 16)
                return v.bn_stats(stats[0:ROWS[c], c, :], h32[0:ROWS[c], c, :])

            dve.wait_ge(edges_in, 16 * 3)
            v.scalar_tensor_tensor(out=TF[:, 1, :], in0=raw[:, 1, :], scalar=float(R), in1=raw[:, 2, :],
                                   op0=ALU.mult, op1=ALU.add)
            row_stats(0)
            dve.wait_ge(w_high_in, 2)
            link(v.tensor_tensor(TF[:, 3, :], raw[:, 3, :].bitcast(F32), TF[:, 2, :], ALU.subtract))
            v.tensor_scalar(TF[:, 3, :], TF[:, 3, :], LO_SCALE, None, ALU.mult).then_inc(efields, 1)
            for c in range(1, NT):
                i = row_stats(c)
            dve.wait_ge(first_in, 1)
            r = firsts(0)
            link(i)
            for c in range(NT):
                i = v.bn_aggr(mv[0:ROWS[c], c, :], stats[0:ROWS[c], c, :])
            i.then_inc(xstat, 1)
            link(v.tensor_reduce(dmin, dst_t, AX.X, ALU.min))
            v.tensor_tensor(from_max[:, :, :], blk3, dmax3, ALU.subtract)
            link(v.tensor_tensor(from_min[:, :, :], blk3, dmin.unsqueeze(2).broadcast_to([EP, EG, NB]), ALU.subtract))
            link(v.scalar_tensor_tensor(out=ov[:, :, :], in0=from_min[:, :, :], scalar=float(-BW), in1=ind[:, :, :],
                                        op0=ALU.is_gt, op1=ALU.is_gt))
            v.tensor_scalar(from_max[:, :, :], from_max[:, :, :], float(1 - BW), None, ALU.max)
            v.tensor_scalar(from_min[:, :, :], from_min[:, :, :], 0.0, None, ALU.min)
            dve.wait_ge(xrstd, 1)
            v.scalar_tensor_tensor(out=nmr, in0=mv[:, :, 0], scalar=-1.0, in1=rstd, op0=ALU.mult,
                                   op1=ALU.mult).then_inc(xnmr, 1)

            def pick(b, first):
                if b >= SB:
                    dve.wait_ge(oh_act, b - SB + 1)
                off = key_off[0:EK, b, :].unsqueeze(2).broadcast_to([EK, 4, SL])
                v.tensor_tensor(slot[0:EK, b % SB, :, :], fields[0:EK, :, bass.ds(first, SL)], off,
                                ALU.subtract).then_inc(gath, 1)

            def build(b):
                dve.wait_ge(gath, b + 1)
                f = slot[0:EK, b % SB, :, :]
                v.tensor_tensor(keq[0:EK, b % 2, :, :], iota_win[0:EK, :, :],
                                f[:, 1, :].unsqueeze(2).broadcast_to([EK, SL, WK]), ALU.is_equal).then_inc(keq_in, 1)
                ring_free(dve, b)
                if (b + 1) % HB:
                    pick(b + 1, r[(b + 1) % HB])
                oh, wk = ring(b)
                for j in range(SL - 1):
                    v.tensor_scalar(oh[0:EK, j, :], iota_src[0:EK, :], f[:, 0, j:j + 1], None, ALU.is_equal)
                dve.wait_ge(keq_in, b + 1)
                v.tensor_tensor(wk[0:EK, :, :].rearrange("e s (h n) -> e s h n", h=2),
                                keq[0:EK, b % 2, :, :].unsqueeze(2).broadcast_to([EK, SL, 2, WK]),
                                f[:, 2:4, :].rearrange("e h s -> e s h").unsqueeze(3).broadcast_to([EK, SL, 2, WK]),
                                ALU.mult).then_inc(blk_in, 1)

            def low_A(q):
                dve.wait_ge(AT_a, q + 1)
                if q >= 2:
                    dve.wait_ge(G_ps, 2 * (q - 1))
                v.tensor_tensor(AT_lo[:, q % 2, :, :], A32[:, :, :], f32(AT_hi[:, q % 2, :, :]),
                                ALU.subtract).then_inc(AT_b, 1)

            def evac_A(q):
                dve.wait_ge(A_lo_ev, q + 1)
                v.tensor_tensor(A32[:, :, :], psA[:, :, 0:HC], A32[:, :, :], ALU.add).then_inc(A_ev, 1)

            def evac_G(q, banks):
                h, k0, k1 = q % 2, 2 * banks[0], 2 * banks[-1] + 2
                dve.wait_ge(G_a, 2 * q + banks[-1] + 1)
                v.tensor_tensor(G_lo[:, k0:k1, :, h * HD:(h + 1) * HD],
                                G_banks(q)[:, k0:k1, :].rearrange("p k (d r) -> p k r d", r=R),
                                f32(G_hi[:, k0:k1, :, h * HD:(h + 1) * HD]), ALU.subtract).then_inc(G_b, len(banks))

            def evac_D(q):
                h = q % 2
                dve.wait_ge(D_ps, q + 1)
                if q % 2 == 0 and q >= 2:
                    dve.wait_ge(W_ps, q // 2)
                v.tensor_copy(D4[:, h * HD:(h + 1) * HD], psX[0:R, 0:HD]).then_inc(D_ev, 1)

            def inv_deg(c):
                m = ROWS[c]
                dve.wait_ge(deg_ps, c + 1)
                v.tensor_scalar(rdeg[0:m, c:c + 1], psG[0:m, 0, 0:1], 1.0, None, ALU.max).then_inc(deg_m, 1)
                dve.wait_ge(deg_m, c + 1)
                v.reciprocal(rdeg[0:m, c:c + 1], rdeg[0:m, c:c + 1]).then_inc(deg_ev, 1)

            def ln1_a(c):
                m = ROWS[c]
                dve.wait_ge(W_ps, c + 1)
                dve.wait_ge(deg_ev, c + 1)
                if c >= 1:
                    dve.wait_ge(x1_in, c)
                v.scalar_tensor_tensor(out=tbuf[0:m, :], in0=psX[0:m, :], scalar=rdeg[0:m, c:c + 1],
                                       in1=x1[0:m, c, :], op0=ALU.mult, op1=ALU.add).then_inc(t_out, 1)
                dve.wait_ge(t_out, 2 * c + 1)
                v.bn_stats(st1[0:m], tbuf[0:m, :]).then_inc(t_out, 1)
                dve.wait_ge(t_out, 2 * c + 2)
                v.bn_aggr(mv1[0:m], st1[0:m]).then_inc(ln1_v, 1)

            def ln1_b(c):
                m = ROWS[c]
                dve.wait_ge(ln1_r, c + 1)
                v.scalar_tensor_tensor(out=nm1[0:m], in0=mv1[0:m, 0:1], scalar=-1.0, in1=rs1[0:m],
                                       op0=ALU.mult, op1=ALU.mult).then_inc(ln1_n, 1)

            def turn_low(c):
                m = ROWS[c]
                dve.wait_ge(xT_a, c + 1)
                v.tensor_tensor(x1T_lo[:, :, c * P:c * P + m],
                                psX[:, :].rearrange("p (k m) -> p k m", k=KD)[:, :, 0:m],
                                f32(x1T_hi[:, :, c * P:c * P + m]), ALU.subtract).then_inc(xT_b, 1)

            def general(q):
                with dve.If(flag > 0):
                    dve.wait_ge(blk_used, HB * (q + 1))
                    with dve.Fori(0, ET) as t:
                        v.tensor_copy(gslot[0:EK, :], fields[0:EK, :, bass.ds(t, 1)].squeeze(2)).then_inc(gen_m, 1)
                        dve.wait_ge(gen_m, t * 2 + (q * ET * 2 + 1))
                        v.tensor_scalar(gslot[0:EK, 1:2], gslot[0:EK, 1:2], float(q * HC), None,
                                        ALU.subtract).then_inc(gen_m, 1)
                        dve.wait_ge(gen_m, t * 2 + (q * ET * 2 + 2))
                        v.tensor_scalar(onehot[0:EK, 0, :], iota_src[0:EK, :], gslot[0:EK, 0:1], None, ALU.is_equal)
                        for part in range(2):
                            i = v.tensor_scalar(gkey[0:EK, part * HC:(part + 1) * HC], iota_src[0:EK, 0:HC],
                                                gslot[0:EK, 1:2], gslot[0:EK, 2 + part:3 + part],
                                                ALU.is_equal, ALU.mult)
                        i.then_inc(gen_in, 1)
                        dve.wait_ge(gen_used, t + (q * ET + 1))

            def self_low(c):
                m = ROWS[c]
                dve.wait_ge(hT_a, c + 1)
                v.tensor_tensor(hT[c % 2][:, 1, :, 0:m], psG[:, 0, :].rearrange("p (k m) -> p k m", k=KD)[:, :, 0:m],
                                f32(hT[c % 2][:, 0, :, 0:m]), ALU.subtract).then_inc(hT_b, 1)

            def self_add(c):
                m = ROWS[c]
                dve.wait_ge(self_ps, c + 1)
                dve.wait_ge(h_bs, c + 1)
                v.tensor_tensor(x1[0:m, c, :], self_bank(c)[0:m], x1[0:m, c, :], ALU.add).then_inc(self_ev, 1)

            dve.wait_ge(eT, 1)
            for b in range(2):
                i = v.tensor_copy(
                    fields[0:EK, 2 * b:2 * b + 2, 0:ET].rearrange("e f (p g) -> e f g p", g=EG),
                    psA[0:EK, b, 0:2 * ET].rearrange("e (f g p) -> e f g p", f=2, g=EG))
                i.then_inc(turned, 1)

            dve.wait_ge(first_in, 2)
            link(v.tensor_tensor(uu[:, :, :], fcol[0:EP, :].unsqueeze(1).broadcast_to([EP, EG, NB]),
                                 negt.unsqueeze(2).broadcast_to([EP, EG, NB]), ALU.add))
            v.scalar_tensor_tensor(out=miss[:, 0, :, :], in0=uu[:, :, :], scalar=0.5, in1=ov[:, :, :],
                                   op0=ALU.is_gt, op1=ALU.mult)
            v.scalar_tensor_tensor(out=from_max[:, :, :], in0=uu[:, :, :], scalar=float(RATE), in1=from_max[:, :, :],
                                   op0=ALU.mult, op1=ALU.subtract)
            link(v.scalar_tensor_tensor(out=from_min[:, :, :], in0=uu[:, :, :], scalar=float(-RATE),
                                        in1=from_min[:, :, :], op0=ALU.mult, op1=ALU.add))
            v.scalar_tensor_tensor(out=miss[:, 1, :, :], in0=from_max[:, :, :], scalar=LEAD - 0.5, in1=ov[:, :, :],
                                   op0=ALU.is_gt, op1=ALU.mult)
            link(v.scalar_tensor_tensor(out=miss[:, 2, :, :], in0=from_min[:, :, :], scalar=LAG + 0.5, in1=ov[:, :, :],
                                        op0=ALU.is_gt, op1=ALU.mult))
            v.tensor_reduce(vsum, miss[:, :, :, :].rearrange("p a g b -> p (a g b)"), AX.X, ALU.add).then_inc(viol, 1)
            self_low(0)
            low_part(dve, 1)
            dve.wait_ge(iotas, 1)
            dve.wait_ge(turned, 2)
            pick(0, r[0])
            build(0)
            dve.wait_ge(vcnt, 1)
            v.tensor_copy(f_i32[:, NB:NB + 1], psA[:, NT - 1, 0:1]).then_inc(regs_in, 1)
            dve.wait_ge(regs_in, 1)
            flag = dve.value_load(f_i32[0:1, NB:NB + 1], min_val=0, max_val=1 << 20)
            self_low(1)
            build(1)
            self_add(0)
            self_low(2)
            build(2)
            r = firsts(1)
            pick(HB, r[0])
            self_add(1)
            self_low(3)
            build(3)
            self_add(2)
            self_low(4)
            general(0)
            build(HB)
            evac_A(0)
            build(HB + 1)
            following = firsts(2)
            low_A(0)
            build(HB + 2)
            r = following
            pick(2 * HB, r[0])
            build(HB + 3)
            self_add(NT - 2)
            self_add(NT - 1)
            v.memset(f32(x1T_hi[:, :, N:NP]), 0.0)
            v.memset(f32(x1T_lo[:, :, N:NP]), 0.0).then_inc(xpad, 1)
            general(1)
            for q in range(NQ):
                c, b = q // 2, HB * (q + 2)
                after, more = q + 1 < NQ, q + 2 < NQ
                if q % 2 == 0:
                    if more:
                        build(b)
                    evac_G(q, [0])
                    evac_A(q + 1)
                    if more:
                        build(b + 1)
                        following = firsts(q + 3)
                    if q >= 2:
                        turn_low(c - 1)
                    evac_G(q, [1])
                    low_A(q + 1)
                    evac_D(q)
                    if more:
                        build(b + 2)
                else:
                    evac_D(q)
                    evac_G(q, [0, 1])
                    if more:
                        build(b)
                        evac_A(q + 1)
                        build(b + 1)
                        if q + 3 < NQ:
                            following = firsts(q + 3)
                        inv_deg(c)
                        low_A(q + 1)
                        build(b + 2)
                        if q + 3 < NQ:
                            r = following
                            pick(HB * (q + 3), r[0])
                        ln1_a(c)
                    elif after:
                        evac_A(q + 1)
                        inv_deg(c)
                        low_A(q + 1)
                        ln1_a(c)
                        ln1_b(c)
                if more:
                    if q % 2 == 0:
                        r = following
                        pick(HB * (q + 3), r[0])
                    build(b + 3)
                    if q % 2 == 1:
                        ln1_b(c)
                    general(q + 2)
            for u in range(U_REL, U_W1):
                low_part(dve, u)
            inv_deg(NT - 1)
            ln1_a(NT - 1)
            ln1_b(NT - 1)
            i = 0
            for g0, n in FG:
                for f in range(KF):
                    if i == NT:
                        turn_low(NT - 1)
                    dve.wait_ge(U_g, i + 1)
                    v.tensor_copy(u_hi[:, f, g0:g0 + n], u32[:, i % 2, 0:n]).then_inc(U_a, 1)
                    dve.wait_ge(U_a, i + 1)
                    v.tensor_tensor(u_lo[:, f, g0:g0 + n], u32[:, i % 2, 0:n], f32(u_hi[:, f, g0:g0 + n]),
                                    ALU.subtract).then_inc(U_b, 1)
                    i += 1
            for c in range(NT):
                m, b = ROWS[c], c % 2
                dve.wait_ge(Y_ps, c + 1)
                dve.wait_ge(x1b, c + 1)
                link(v.tensor_tensor(t2buf[0:m, b, :], ybank(c)[0:m], x1[0:m, c, :], ALU.add))
                link(v.bn_stats(st2[0:m, b, :], t2buf[0:m, b, :]))
                v.bn_aggr(mv2[0:m, b, :], st2[0:m, b, :]).then_inc(ln2_v, 1)
                dve.wait_ge(ln2_v, c + 1)
                v.scalar_tensor_tensor(out=t2buf[0:m, b, :], in0=t2buf[0:m, b, :], scalar=mv2[0:m, b, 0:1],
                                       in1=g2_bc[0:m, :], op0=ALU.subtract, op1=ALU.mult).then_inc(y_g, 1)
                dve.wait_ge(y_g, c + 1)
                dve.wait_ge(ln2_r, c + 1)
                if c >= 2:
                    dve.wait_ge(out_done[b], 16 * (c // 2))
                v.scalar_tensor_tensor(out=ybuf[0:m, b, :], in0=t2buf[0:m, b, :], scalar=rs2[0:m, b:b + 1],
                                       in1=x_again[0:m, c, :], op0=ALU.mult, op1=ALU.add).then_inc(y_out, 1)

        @block.tensor
        def _(pe):
            def mm(o, l, r, start, stop=False):
                return nc.tensor.matmul(o, l, r, start=start, stop=stop, skip_group_check=True)

            pe.wait_ge(blk_iotas, 1)
            pe.wait_ge(find, 1)
            for g in range(EG):
                i = mm(psX[:, 0:NB], ones[0:EP, :], ind[:, g, :], g == 0, g == EG - 1)
            i.then_inc(fcnt, 1)
            pe.wait_ge(iotas, 1)
            pe.wait_ge(efields, 1)
            pe.wait_ge(srcs, 1)
            for f in range(4):
                for g in range(EG):
                    c0 = (f % 2) * ET + g * EP
                    i = nc.tensor.transpose(psA[0:EK, f // 2, c0:c0 + EP], TF[:, f, g * EK:(g + 1) * EK],
                                            ident[0:EP, 0:EP])
            i.then_inc(eT, 1)

            def turn_h(c):
                m = ROWS[c]
                pe.wait_ge(h_act, c + 1)
                if c >= 1:
                    pe.wait_ge(hT_b, c)
                for k in range(KD):
                    i = nc.tensor.transpose(psG[:, 0, k * P:k * P + m], h32[0:m, c, k * P:(k + 1) * P],
                                            ident[0:m, 0:m])
                i.then_inc(hT_ps, 1)

            def self_product(c):
                m = ROWS[c]
                pe.wait_ge(hT_b, c + 1)
                pe.wait_ge(*split(0))
                pe.wait_ge(*split(1))
                if c >= 2:
                    pe.wait_ge(self_ev, c - 1)
                t, o = hT[c % 2], self_bank(c)[0:m]
                for k in range(KD):
                    mm(o, t[:, 0, k, 0:m], wself_hi[:, k, :], k == 0)
                    mm(o, t[:, 1, k, 0:m], wself_hi[:, k, :], False)
                    i = mm(o, t[:, 0, k, 0:m], wself_lo[:, k, :], False, k == KD - 1)
                i.then_inc(self_ps, 1)

            def build(q, blocks):
                for i in blocks:
                    b = HB * q + i
                    pe.wait_ge(blk_in, b + 1)
                    pe.wait_ge(oh_act, b + 1)
                    for j in range(SL):
                        oh, wk = ring(b)
                        lo, hi = WINDOW[j]
                        c0, c1 = (i * BW + lo) * R, (i * BW + hi) * R
                        keys = wk[0:EK, j, :].rearrange("e (h n) -> e h n", h=2)
                        keys = keys[:, :, (lo - W0[j]) * R:(hi - W0[j]) * R]
                        for t in range(NT):
                            o = psA[:, t, :].rearrange("p (h n) -> p h n", h=2)[:, :, c0:c1]
                            last = mm(o, oh[0:EK, j, t * P:(t + 1) * P], keys,
                                      i == 0 and j == 0, i == HB - 1 and j == SL - 1)
                    last.then_inc(blk_used, 1)

            def finish_A(q):
                with pe.If(flag > 0):
                    pe.wait_ge(gen_in, q * ET + 1)
                    general_tile(True).then_inc(gen_used, 1)
                    with pe.Fori(1, ET) as t:
                        pe.wait_ge(gen_in, t + (q * ET + 1))
                        general_tile(False).then_inc(gen_used, 1)
                mm(psA[0:64, NT - 1, 0:2], zeros[:, :], zeros[:, 0:2], False, True).then_inc(A_ps, 1)

            def general_tile(start):
                for t in range(NT):
                    i = mm(psA[:, t, :], onehot[0:EK, 0, t * P:(t + 1) * P], gkey[0:EK], start)
                return i

            def G_hi_A(q, k):
                if 1 <= q < NQ - 1:
                    pe.wait_ge(G_b, 2 * (q - 1) + k // 2 + 1)
                pe.wait_ge(AT_a, q + 1)
                o = G_banks(q)[:, k, :]
                for s in range(NT):
                    m = ROWS[s]
                    mm(o, h_hi[0:m, s, k * P:(k + 1) * P], AT_hi[0:m, q % 2, s, :], k % 2 == 0 and s == 0)
                    mm(o, h_lo[0:m, s, k * P:(k + 1) * P], AT_hi[0:m, q % 2, s, :], False)

            def G_lo_A(q, k):
                pe.wait_ge(AT_b, q + 1)
                o = G_banks(q)[:, k, :]
                for s in range(NT):
                    m = ROWS[s]
                    last = mm(o, h_hi[0:m, s, k * P:(k + 1) * P], AT_lo[0:m, q % 2, s, :], False, s == NT - 1)
                if k % 2 == 1:
                    last.then_inc(G_ps, 1)

            def degrees(q):
                pe.wait_ge(A_s, q + 1)
                if q >= 1:
                    pe.wait_ge(D_ev, q)
                for r in range(R):
                    i = mm(psX[0:R, 0:HD], select[:, r, :], A_sum[:, :].rearrange("p (d r) -> p r d", r=R)[:, r, :],
                           r == 0, r == R - 1)
                i.then_inc(D_ps, 1)

            def turn_x1(c):
                m = ROWS[c]
                pe.wait_ge(x1_in, c + 1)
                for k in range(KD):
                    i = nc.tensor.transpose(psX[:, k * P:k * P + m], x1[0:m, c, k * P:(k + 1) * P], ident[0:m, 0:m])
                i.then_inc(xT_ps, 1)

            def ffn1_hi(i, group, tiles, start):
                g0, n = group
                f, o = i % KF, U_bank(i)[:, 0:n]
                for k in tiles:
                    w = W1_hi[:, k, f * P:(f + 1) * P]
                    mm(o, w, x1T_hi[:, k, g0:g0 + n], start and k == 0)
                    mm(o, w, x1T_lo[:, k, g0:g0 + n], False)

            def rel_product(c):
                m = ROWS[c]
                pe.wait_ge(D_ev, 2 * c + 2)
                mm(psX[0:m, :], D4[:, 0:m], brel_sb[:, :], True)
                pe.wait_ge(G_a, 4 * c + 4)
                for r in range(R):
                    if c == 0:
                        pe.wait_ge(*split(U_SELF + 2 * r + 1))
                    for k in range(KD):
                        mm(psX[0:m, :], G_hi[:, k, r, 0:m], wrel_hi[:, r, k, :], False)
                        mm(psX[0:m, :], G_hi[:, k, r, 0:m], wrel_lo[:, r, k, :], False)
                pe.wait_ge(G_b, 4 * c + 4)
                mm(psG[0:m, 0, 0:1], D4[:, 0:m], ones[0:R, 0:1], True, True).then_inc(deg_ps, 1)
                for r in range(R):
                    for k in range(KD):
                        i = mm(psX[0:m, :], G_lo[:, k, r, 0:m], wrel_hi[:, r, k, :], False,
                               r == R - 1 and k == KD - 1)
                i.then_inc(W_ps, 1)

            turn_h(0)
            turn_h(1)
            pe.wait_ge(viol, 1)
            pe.wait_ge(turned, 2)
            mm(psA[:, NT - 1, 0:1], ones[0:EP, :], vsum, True, True).then_inc(vcnt, 1)
            self_product(0)
            pe.wait_ge(regs_in, 1)
            flag = pe.value_load(f_i32[0:1, NB:NB + 1], min_val=0, max_val=1 << 20)
            for i in range(HB):
                build(0, range(i, i + 1))
                if i + 2 < NT:
                    turn_h(i + 2)
                if i + 1 < HB:
                    self_product(i + 1)
            finish_A(0)
            self_product(NT - 1)
            for q in range(NQ):
                c, after = q // 2, q + 1 < NQ
                pe.wait_ge(A_ev, q + 1)
                if q % 2 == 0:
                    build(q + 1, range(0, 2))
                    if q == 0:
                        pe.wait_ge(h_los, NT)
                    else:
                        pe.wait_ge(deg_ev, c)
                    for k in range(0, 2):
                        G_hi_A(q, k)
                        G_lo_A(q, k)
                    build(q + 1, range(2, 4))
                    finish_A(q + 1)
                    if q == 0:
                        pe.wait_ge(self_ev, NT)
                    for k in range(2, KD):
                        G_hi_A(q, k)
                        G_lo_A(q, k)
                        if k == 2 and q >= 2:
                            turn_x1(c - 1)
                else:
                    if after:
                        build(q + 1, range(0, 1))
                    for k in range(0, 2):
                        G_hi_A(q, k)
                    if after:
                        build(q + 1, range(1, 2))
                    if q >= 3:
                        pe.wait_ge(xT_b, c)
                    degrees(q - 1)
                    for k in range(2, KD):
                        G_hi_A(q, k)
                    for k in range(KD):
                        G_lo_A(q, k)
                    degrees(q)
                    if after:
                        build(q + 1, range(2, 4))
                        finish_A(q + 1)
                    else:
                        pe.wait_ge(w_hi, U_REL + KD - 1)
                        for f in range(EARLY):
                            ffn1_hi(f, FG[0], range(0, KD - 1), True)
                    rel_product(c)
            i = 0
            for g in range(len(FG)):
                if g == 1:
                    pe.wait_ge(xT_b, NT)
                    pe.wait_ge(xpad, 1)
                for f in range(KF):
                    if i == 0:
                        pe.wait_ge(*split(U_W1 - 1))
                    if i == NT:
                        turn_x1(NT - 1)
                    if i >= NT:
                        pe.wait_ge(U_g, i - NT + 1)
                    if i < EARLY:
                        ffn1_hi(i, FG[g], range(KD - 1, KD), False)
                    else:
                        ffn1_hi(i, FG[g], range(KD), True)
                    g0, n = FG[g]
                    for k in range(KD):
                        last = mm(U_bank(i)[:, 0:n], W1_lo[:, k, f * P:(f + 1) * P], x1T_hi[:, k, g0:g0 + n], False,
                                  k == KD - 1)
                    last.then_inc(U_ps, 1)
                    i += 1
            pe.wait_ge(*split(NU - 1))
            for c in range(NT):
                m = ROWS[c]
                pe.wait_ge(U_b, KF if c < 3 else 2 * KF)
                if c >= 3:
                    pe.wait_ge(ln2_v, c - 2)
                o = ybank(c)[0:m]
                for f in range(KF):
                    uh, ul = u_hi[:, f, c * P:c * P + m], u_lo[:, f, c * P:c * P + m]
                    mm(o, uh, W2_hi[:, f, :], f == 0)
                    mm(o, ul, W2_hi[:, f, :], False)
                    last = mm(o, uh, W2_lo[:, f, :], False, f == KF - 1)
                last.then_inc(Y_ps, 1)


_INS = ["x", "src", "dst", "edge_type_4", "edge_weight", "L0_gnn_W_self", "L0_gnn_b_self", "L0_gnn_W_rel",
        "L0_gnn_b_rel", "L0_gnn_ln1_g", "L0_gnn_ln1_b", "L0_gnn_ln2_g", "L0_gnn_ln2_b", "L0_gnn_W_ffn1",
        "L0_gnn_b_ffn1", "L0_gnn_W_ffn2", "L0_gnn_b_ffn2"]


def kernel(**inputs):
    import numpy as np
    import concourse.bacc as bacc
    from concourse.bass_utils import run_bass_kernel_spmd as run

    nc = bacc.Bacc("TRN2", target_bir_lowering=False, num_devices=1)
    arrays, args = {}, []
    for name in _INS:
        a = np.ascontiguousarray(inputs[name])
        arrays[f"in_{name}"] = a
        args.append(nc.dram_tensor(f"in_{name}", a.shape, mybir.dt.from_np(a.dtype), kind="ExternalInput").ap())
    shape = inputs["x"].shape
    args.append(nc.dram_tensor("out_0", shape, F32, kind="ExternalOutput").ap())
    gnn_layer(nc, *args)
    r = run(nc, [arrays], core_ids=[0])
    return r.results[0]["out_0"]
```
